# Optimizing a Trainium2 kernel written in Bass

```python
import numpy as np
import jax
import jax.numpy as jnp

def _softmax(x, axis=-1):
    return jax.nn.softmax(x, axis=axis)

def _gelu(x):
    return jax.nn.gelu(x, approximate=True)

def _silu(x):
    return jax.nn.silu(x)

def _sigmoid(x):
    return jax.nn.sigmoid(x)

def _layernorm(x, axis=-1, eps=1e-05):
    m = jnp.mean(x, axis=axis, keepdims=True)
    v = jnp.var(x, axis=axis, keepdims=True)
    return (x - m) / jnp.sqrt(v + eps)

def _scatter_add(tgt, idx, src, axis=0):
    return tgt.at[idx].add(src)

def _segment_sum(src, seg, n):
    return jax.ops.segment_sum(src, seg, n)
kernel_name = 'mk_pixart_seq_d2_seqx_r8_a0fade'

def setup_inputs(seed: int=0):
    np.random.seed(seed)
    _w = jnp.asarray

    def _rec_inputs():
        import jax
        import jax.numpy as jnp
        _rk = jax.random.key(seed)
        x = -0.0005207 + 1.001 * jax.random.normal(jax.random.fold_in(_rk, 1), (8, 128, 128), jnp.float32)
        _lenS = 128 - jax.random.randint(jax.random.fold_in(_rk, 7), (8,), 0, max(1, 128 // 4) + 1, jnp.int32)
        _lenS2 = 128 - jax.random.randint(jax.random.fold_in(_rk, 8), (8,), 0, max(1, 128 // 4) + 1, jnp.int32)
        cond_1024 = 0.000887014 + 1.03683 * jax.random.normal(jax.random.fold_in(_rk, 11), (8, 128), jnp.float32)
        _ctx_768P = jax.random.normal(jax.random.fold_in(_rk, 12), (8, 16, 96), jnp.float32)
        _ctx_768c = jax.random.dirichlet(jax.random.fold_in(_rk, 512), 0.3 * jnp.ones((16,), jnp.float32), (8, 128))
        _ctx_768t = jnp.einsum('bsk,bkd->bsd', _ctx_768c, _ctx_768P)
        _ctx_768t = _ctx_768t * jax.lax.rsqrt(jnp.mean(jnp.square(_ctx_768t)) + 1e-12) * 0.953939
        ctx_768 = 0.000599585 + 1.00006 * (_ctx_768t + 0.3 * jax.random.normal(jax.random.fold_in(_rk, 612), (8, 128, 96), jnp.float32))
        return (x, cond_1024, ctx_768)
    x, cond_1024, ctx_768 = _rec_inputs()

    def _L0_xcond_setup():
        import jax, jax.numpy as jnp
        import numpy as np
        B, N, M = (2, 128, 64)
        D, H, DH = (128, 16, 64)
        MID = H * DH
        DC = 96
        MULT = 4
        EPS = 1e-05

        def _ln(x, w, b):
            mu = jnp.mean(x, -1, keepdims=True)
            var = jnp.mean((x - mu) ** 2, -1, keepdims=True)
            return (x - mu) * jax.lax.rsqrt(var + EPS) * w + b

        def _sincos(n, d):
            inv = 1.0 / 10000.0 ** (jnp.arange(0, d, 2, dtype=jnp.float32) / d)
            ang = jnp.arange(n, dtype=jnp.float32)[:, None] * inv[None, :]
            return (jnp.sin(ang), jnp.cos(ang))

        def _rope(x, sin, cos):
            s = sin[None, None]
            c = cos[None, None]
            xe = x[..., ::2]
            xo = x[..., 1::2]
            re = xe * c - xo * s
            ro = xe * s + xo * c
            return jnp.stack((re, ro), axis=-1).reshape(x.shape)

        def _heads(t):
            b, n, _ = t.shape
            return t.reshape(b, n, H, DH).transpose(0, 2, 1, 3)

        def _attn(xq, ctx, wq, wkv, wo, bo):
            q = _heads(xq @ wq)
            k, v = jnp.split(ctx @ wkv, 2, axis=-1)
            k = _heads(k)
            v = _heads(v)
            sq, cq = _sincos(q.shape[2], DH)
            sk, ck = _sincos(k.shape[2], DH)
            q = _rope(q, sq, cq)
            k = _rope(k, sk, ck)
            sim = jnp.einsum('bhnd,bhmd->bhnm', q, k) * DH ** (-0.5)
            a = jax.nn.softmax(sim, axis=-1)
            o = jnp.einsum('bhnm,bhmd->bhnd', a, v)
            o = o.transpose(0, 2, 1, 3).reshape(xq.shape[0], xq.shape[1], MID)
            return o @ wo + bo

        def _adaln(x, c, lw, lb, gw, gb, bw, bb):
            g = (c @ gw + gb)[:, None, :]
            bt = (c @ bw + bb)[:, None, :]
            return _ln(x, lw, lb) * (1.0 + g) + bt
        ks = jax.random.split(jax.random.key(seed), 24)
        s = 0.02
        inp = {'x': jax.random.normal(ks[0], (B, N, D), jnp.float32), 'cond': jax.random.normal(ks[1], (B, D), jnp.float32), 'context': jax.random.normal(ks[2], (B, M, DC), jnp.float32), 'ln1_w': jnp.ones((D,), jnp.float32), 'ln1_b': jnp.zeros((D,), jnp.float32), 'g1_w': jax.random.normal(ks[3], (D, D), jnp.float32) * s, 'g1_b': jnp.zeros((D,), jnp.float32), 'b1_w': jax.random.normal(ks[4], (D, D), jnp.float32) * s, 'b1_b': jnp.zeros((D,), jnp.float32), 'ln2_w': jnp.ones((D,), jnp.float32), 'ln2_b': jnp.zeros((D,), jnp.float32), 'g2_w': jax.random.normal(ks[5], (D, D), jnp.float32) * s, 'g2_b': jnp.zeros((D,), jnp.float32), 'b2_w': jax.random.normal(ks[6], (D, D), jnp.float32) * s, 'b2_b': jnp.zeros((D,), jnp.float32), 'sa_wq': jax.random.normal(ks[7], (D, MID), jnp.float32) * s, 'sa_wkv': jax.random.normal(ks[8], (D, 2 * MID), jnp.float32) * s, 'sa_wo': jax.random.normal(ks[9], (MID, D), jnp.float32) * s, 'sa_bo': jnp.zeros((D,), jnp.float32), 'ca_lnc_w': jnp.ones((DC,), jnp.float32), 'ca_lnc_b': jnp.zeros((DC,), jnp.float32), 'ca_wq': jax.random.normal(ks[10], (D, MID), jnp.float32) * s, 'ca_wkv': jax.random.normal(ks[11], (DC, 2 * MID), jnp.float32) * s, 'ca_wo': jax.random.normal(ks[12], (MID, D), jnp.float32) * s, 'ca_bo': jnp.zeros((D,), jnp.float32), 'ff_w1': jax.random.normal(ks[13], (D, MULT * D), jnp.float32) * s, 'ff_b1': jnp.zeros((MULT * D,), jnp.float32), 'ff_w2': jax.random.normal(ks[14], (MULT * D, D), jnp.float32) * s, 'ff_b2': jnp.zeros((D,), jnp.float32)}
        return inp
    _L0_xcond_all = _L0_xcond_setup()
    _L0_xcond_in = {k: v for k, v in _L0_xcond_all.items() if k in ('ln1_w', 'ln1_b', 'g1_w', 'g1_b', 'b1_w', 'b1_b', 'ln2_w', 'ln2_b', 'g2_w', 'g2_b', 'b2_w', 'b2_b', 'sa_wq', 'sa_wkv', 'sa_wo', 'sa_bo', 'ca_lnc_w', 'ca_lnc_b', 'ca_wq', 'ca_wkv', 'ca_wo', 'ca_bo', 'ff_w1', 'ff_b1', 'ff_w2', 'ff_b2')}
    del _L0_xcond_all

    def _L1_xcond_setup():
        import jax, jax.numpy as jnp
        import numpy as np
        B, N, D, H, TD, TL = (4, 128, 128, 16, 96, 77)
        HD = D // H
        EPS = 1e-06

        def _ln(x):
            mu = jnp.mean(x, axis=-1, keepdims=True)
            var = jnp.var(x, axis=-1, keepdims=True)
            return (x - mu) * jax.lax.rsqrt(var + EPS)

        def _modulate(x, shift, scale):
            return x * (1.0 + scale[:, None, :]) + shift[:, None, :]

        def _heads(t):
            return t.reshape(t.shape[0], t.shape[1], H, HD).transpose(0, 2, 1, 3)

        def _attend(q, k, v):
            sim = jnp.einsum('bhid,bhjd->bhij', q, k) * HD ** (-0.5)
            attn = jax.nn.softmax(sim, axis=-1)
            out = jnp.einsum('bhij,bhjd->bhid', attn, v)
            return out.transpose(0, 2, 1, 3).reshape(out.shape[0], -1, D)
        key = jax.random.key(seed)
        ks = jax.random.split(key, 16)
        s = 0.02
        return {'x': jax.random.normal(ks[0], (B, N, D), jnp.float32), 'c': jax.random.normal(ks[1], (B, D), jnp.float32), 'text_embed': jax.random.normal(ks[2], (B, TL, TD), jnp.float32), 'W_ada': jax.random.normal(ks[3], (D, 6 * D), jnp.float32) * s, 'b_ada': jnp.zeros((6 * D,), jnp.float32), 'W_qkv': jax.random.normal(ks[4], (D, 3 * D), jnp.float32) * s, 'b_qkv': jnp.zeros((3 * D,), jnp.float32), 'W_proj': jax.random.normal(ks[5], (D, D), jnp.float32) * s, 'b_proj': jnp.zeros((D,), jnp.float32), 'W_ctx': jax.random.normal(ks[6], (TD, D), jnp.float32) * s, 'b_ctx': jnp.zeros((D,), jnp.float32), 'W_q': jax.random.normal(ks[7], (D, D), jnp.float32) * s, 'W_k': jax.random.normal(ks[8], (D, D), jnp.float32) * s, 'W_v': jax.random.normal(ks[9], (D, D), jnp.float32) * s, 'W_out': jax.random.normal(ks[10], (D, D), jnp.float32) * s, 'b_out': jnp.zeros((D,), jnp.float32), 'W_fc1': jax.random.normal(ks[11], (D, 4 * D), jnp.float32) * s, 'b_fc1': jnp.zeros((4 * D,), jnp.float32), 'W_fc2': jax.random.normal(ks[12], (4 * D, D), jnp.float32) * s, 'b_fc2': jnp.zeros((D,), jnp.float32)}
    _L1_xcond_all = _L1_xcond_setup()
    _L1_xcond_in = {k: v for k, v in _L1_xcond_all.items() if k in ('W_ada', 'b_ada', 'W_qkv', 'b_qkv', 'W_proj', 'b_proj', 'W_ctx', 'b_ctx', 'W_q', 'W_k', 'W_v', 'W_out', 'b_out', 'W_fc1', 'b_fc1', 'W_fc2', 'b_fc2')}
    del _L1_xcond_all
    return {'x': x, 'cond_1024': cond_1024, 'ctx_768': ctx_768, 'L0_xcond_ln1_w': _L0_xcond_in['ln1_w'], 'L0_xcond_ln1_b': _L0_xcond_in['ln1_b'], 'L0_xcond_g1_w': _L0_xcond_in['g1_w'], 'L0_xcond_g1_b': _L0_xcond_in['g1_b'], 'L0_xcond_b1_w': _L0_xcond_in['b1_w'], 'L0_xcond_b1_b': _L0_xcond_in['b1_b'], 'L0_xcond_ln2_w': _L0_xcond_in['ln2_w'], 'L0_xcond_ln2_b': _L0_xcond_in['ln2_b'], 'L0_xcond_g2_w': _L0_xcond_in['g2_w'], 'L0_xcond_g2_b': _L0_xcond_in['g2_b'], 'L0_xcond_b2_w': _L0_xcond_in['b2_w'], 'L0_xcond_b2_b': _L0_xcond_in['b2_b'], 'L0_xcond_sa_wq': _L0_xcond_in['sa_wq'], 'L0_xcond_sa_wkv': _L0_xcond_in['sa_wkv'], 'L0_xcond_sa_wo': _L0_xcond_in['sa_wo'], 'L0_xcond_sa_bo': _L0_xcond_in['sa_bo'], 'L0_xcond_ca_lnc_w': _L0_xcond_in['ca_lnc_w'], 'L0_xcond_ca_lnc_b': _L0_xcond_in['ca_lnc_b'], 'L0_xcond_ca_wq': _L0_xcond_in['ca_wq'], 'L0_xcond_ca_wkv': _L0_xcond_in['ca_wkv'], 'L0_xcond_ca_wo': _L0_xcond_in['ca_wo'], 'L0_xcond_ca_bo': _L0_xcond_in['ca_bo'], 'L0_xcond_ff_w1': _L0_xcond_in['ff_w1'], 'L0_xcond_ff_b1': _L0_xcond_in['ff_b1'], 'L0_xcond_ff_w2': _L0_xcond_in['ff_w2'], 'L0_xcond_ff_b2': _L0_xcond_in['ff_b2'], 'L1_xcond_W_ada': _L1_xcond_in['W_ada'], 'L1_xcond_b_ada': _L1_xcond_in['b_ada'], 'L1_xcond_W_qkv': _L1_xcond_in['W_qkv'], 'L1_xcond_b_qkv': _L1_xcond_in['b_qkv'], 'L1_xcond_W_proj': _L1_xcond_in['W_proj'], 'L1_xcond_b_proj': _L1_xcond_in['b_proj'], 'L1_xcond_W_ctx': _L1_xcond_in['W_ctx'], 'L1_xcond_b_ctx': _L1_xcond_in['b_ctx'], 'L1_xcond_W_q': _L1_xcond_in['W_q'], 'L1_xcond_W_k': _L1_xcond_in['W_k'], 'L1_xcond_W_v': _L1_xcond_in['W_v'], 'L1_xcond_W_out': _L1_xcond_in['W_out'], 'L1_xcond_b_out': _L1_xcond_in['b_out'], 'L1_xcond_W_fc1': _L1_xcond_in['W_fc1'], 'L1_xcond_b_fc1': _L1_xcond_in['b_fc1'], 'L1_xcond_W_fc2': _L1_xcond_in['W_fc2'], 'L1_xcond_b_fc2': _L1_xcond_in['b_fc2']}

def reference(x, cond_1024, ctx_768, L0_xcond_ln1_w, L0_xcond_ln1_b, L0_xcond_g1_w, L0_xcond_g1_b, L0_xcond_b1_w, L0_xcond_b1_b, L0_xcond_ln2_w, L0_xcond_ln2_b, L0_xcond_g2_w, L0_xcond_g2_b, L0_xcond_b2_w, L0_xcond_b2_b, L0_xcond_sa_wq, L0_xcond_sa_wkv, L0_xcond_sa_wo, L0_xcond_sa_bo, L0_xcond_ca_lnc_w, L0_xcond_ca_lnc_b, L0_xcond_ca_wq, L0_xcond_ca_wkv, L0_xcond_ca_wo, L0_xcond_ca_bo, L0_xcond_ff_w1, L0_xcond_ff_b1, L0_xcond_ff_w2, L0_xcond_ff_b2, L1_xcond_W_ada, L1_xcond_b_ada, L1_xcond_W_qkv, L1_xcond_b_qkv, L1_xcond_W_proj, L1_xcond_b_proj, L1_xcond_W_ctx, L1_xcond_b_ctx, L1_xcond_W_q, L1_xcond_W_k, L1_xcond_W_v, L1_xcond_W_out, L1_xcond_b_out, L1_xcond_W_fc1, L1_xcond_b_fc1, L1_xcond_W_fc2, L1_xcond_b_fc2):
    import jax
    import jax.numpy as jnp

    def _L0_xcond_ref(x, cond, context, ln1_w, ln1_b, g1_w, g1_b, b1_w, b1_b, ln2_w, ln2_b, g2_w, g2_b, b2_w, b2_b, sa_wq, sa_wkv, sa_wo, sa_bo, ca_lnc_w, ca_lnc_b, ca_wq, ca_wkv, ca_wo, ca_bo, ff_w1, ff_b1, ff_w2, ff_b2):
        import jax, jax.numpy as jnp
        import numpy as np
        B, N, M = (2, 128, 64)
        D, H, DH = (128, 16, 64)
        MID = H * DH
        DC = 96
        MULT = 4
        EPS = 1e-05

        def _ln(x, w, b):
            mu = jnp.mean(x, -1, keepdims=True)
            var = jnp.mean((x - mu) ** 2, -1, keepdims=True)
            return (x - mu) * jax.lax.rsqrt(var + EPS) * w + b

        def _sincos(n, d):
            inv = 1.0 / 10000.0 ** (jnp.arange(0, d, 2, dtype=jnp.float32) / d)
            ang = jnp.arange(n, dtype=jnp.float32)[:, None] * inv[None, :]
            return (jnp.sin(ang), jnp.cos(ang))

        def _rope(x, sin, cos):
            s = sin[None, None]
            c = cos[None, None]
            xe = x[..., ::2]
            xo = x[..., 1::2]
            re = xe * c - xo * s
            ro = xe * s + xo * c
            return jnp.stack((re, ro), axis=-1).reshape(x.shape)

        def _heads(t):
            b, n, _ = t.shape
            return t.reshape(b, n, H, DH).transpose(0, 2, 1, 3)

        def _attn(xq, ctx, wq, wkv, wo, bo):
            q = _heads(xq @ wq)
            k, v = jnp.split(ctx @ wkv, 2, axis=-1)
            k = _heads(k)
            v = _heads(v)
            sq, cq = _sincos(q.shape[2], DH)
            sk, ck = _sincos(k.shape[2], DH)
            q = _rope(q, sq, cq)
            k = _rope(k, sk, ck)
            sim = jnp.einsum('bhnd,bhmd->bhnm', q, k) * DH ** (-0.5)
            a = jax.nn.softmax(sim, axis=-1)
            o = jnp.einsum('bhnm,bhmd->bhnd', a, v)
            o = o.transpose(0, 2, 1, 3).reshape(xq.shape[0], xq.shape[1], MID)
            return o @ wo + bo

        def _adaln(x, c, lw, lb, gw, gb, bw, bb):
            g = (c @ gw + gb)[:, None, :]
            bt = (c @ bw + bb)[:, None, :]
            return _ln(x, lw, lb) * (1.0 + g) + bt
        attn_in = _adaln(x, cond, ln1_w, ln1_b, g1_w, g1_b, b1_w, b1_b)
        x = _attn(attn_in, attn_in, sa_wq, sa_wkv, sa_wo, sa_bo) + x
        cross_in = _adaln(x, cond, ln1_w, ln1_b, g1_w, g1_b, b1_w, b1_b)
        ctx_n = _ln(context, ca_lnc_w, ca_lnc_b)
        x = _attn(cross_in, ctx_n, ca_wq, ca_wkv, ca_wo, ca_bo) + x
        ffn_in = _adaln(x, cond, ln2_w, ln2_b, g2_w, g2_b, b2_w, b2_b)
        h = jax.nn.gelu(ffn_in @ ff_w1 + ff_b1, approximate=False)
        x = h @ ff_w2 + ff_b2 + x
        return x

    def _L1_xcond_ref(x, c, text_embed, W_ada, b_ada, W_qkv, b_qkv, W_proj, b_proj, W_ctx, b_ctx, W_q, W_k, W_v, W_out, b_out, W_fc1, b_fc1, W_fc2, b_fc2):
        import jax, jax.numpy as jnp
        import numpy as np
        B, N, D, H, TD, TL = (4, 128, 128, 16, 96, 77)
        HD = D // H
        EPS = 1e-06

        def _ln(x):
            mu = jnp.mean(x, axis=-1, keepdims=True)
            var = jnp.var(x, axis=-1, keepdims=True)
            return (x - mu) * jax.lax.rsqrt(var + EPS)

        def _modulate(x, shift, scale):
            return x * (1.0 + scale[:, None, :]) + shift[:, None, :]

        def _heads(t):
            return t.reshape(t.shape[0], t.shape[1], H, HD).transpose(0, 2, 1, 3)

        def _attend(q, k, v):
            sim = jnp.einsum('bhid,bhjd->bhij', q, k) * HD ** (-0.5)
            attn = jax.nn.softmax(sim, axis=-1)
            out = jnp.einsum('bhij,bhjd->bhid', attn, v)
            return out.transpose(0, 2, 1, 3).reshape(out.shape[0], -1, D)
        mod = jax.nn.silu(c) @ W_ada + b_ada
        sh_msa, sc_msa, sh_x, sc_x, sh_mlp, sc_mlp = jnp.split(mod, 6, axis=-1)
        h1 = _modulate(_ln(x), sh_msa, sc_msa)
        qkv = h1 @ W_qkv + b_qkv
        q, k, v = jnp.split(qkv, 3, axis=-1)
        out = _attend(_heads(q), _heads(k), _heads(v))
        x = x + (out @ W_proj + b_proj)
        h2 = _modulate(_ln(x), sh_x, sc_x)
        ctx = text_embed @ W_ctx + b_ctx
        q = _heads(h2 @ W_q)
        k = _heads(ctx @ W_k)
        v = _heads(ctx @ W_v)
        out = _attend(q, k, v)
        x = x + (out @ W_out + b_out)
        h3 = _modulate(_ln(x), sh_mlp, sc_mlp)
        hidden = jax.nn.gelu(h3 @ W_fc1 + b_fc1, approximate=True)
        x = x + (hidden @ W_fc2 + b_fc2)
        return x
    x = _L0_xcond_ref(x, cond_1024, ctx_768, L0_xcond_ln1_w, L0_xcond_ln1_b, L0_xcond_g1_w, L0_xcond_g1_b, L0_xcond_b1_w, L0_xcond_b1_b, L0_xcond_ln2_w, L0_xcond_ln2_b, L0_xcond_g2_w, L0_xcond_g2_b, L0_xcond_b2_w, L0_xcond_b2_b, L0_xcond_sa_wq, L0_xcond_sa_wkv, L0_xcond_sa_wo, L0_xcond_sa_bo, L0_xcond_ca_lnc_w, L0_xcond_ca_lnc_b, L0_xcond_ca_wq, L0_xcond_ca_wkv, L0_xcond_ca_wo, L0_xcond_ca_bo, L0_xcond_ff_w1, L0_xcond_ff_b1, L0_xcond_ff_w2, L0_xcond_ff_b2)
    x = _L1_xcond_ref(x, cond_1024, ctx_768, L1_xcond_W_ada, L1_xcond_b_ada, L1_xcond_W_qkv, L1_xcond_b_qkv, L1_xcond_W_proj, L1_xcond_b_proj, L1_xcond_W_ctx, L1_xcond_b_ctx, L1_xcond_W_q, L1_xcond_W_k, L1_xcond_W_v, L1_xcond_W_out, L1_xcond_b_out, L1_xcond_W_fc1, L1_xcond_b_fc1, L1_xcond_W_fc2, L1_xcond_b_fc2)
    return x

_drawn_inputs = setup_inputs


def setup_inputs(seed=0):
    import zlib

    import numpy as np

    out = dict(_drawn_inputs(seed))
    spreads = {'L0_xcond_ln1_w': (1.0, 0.6),
     'L0_xcond_ln1_b': (0.0, 0.592),
     'L0_xcond_g1_b': (0.0, 0.8),
     'L0_xcond_b1_b': (0.0, 0.509),
     'L0_xcond_ln2_w': (1.0, 0.6),
     'L0_xcond_ln2_b': (0.0, 0.8),
     'L0_xcond_g2_b': (0.0, 0.8),
     'L0_xcond_b2_b': (0.0, 0.8),
     'L0_xcond_sa_bo': (0.0, 0.1),
     'L0_xcond_ca_lnc_w': (1.0, 0.6),
     'L0_xcond_ca_lnc_b': (0.0, 0.649),
     'L0_xcond_ca_bo': (0.0, 0.1),
     'L0_xcond_ff_b1': (0.0, 0.344),
     'L0_xcond_ff_b2': (0.0, 0.1),
     'L1_xcond_b_ada': (0.0, 0.8),
     'L1_xcond_b_qkv': (0.0, 0.353),
     'L1_xcond_b_proj': (0.0, 0.1),
     'L1_xcond_b_ctx': (0.0, 0.8),
     'L1_xcond_b_out': (0.0, 0.558),
     'L1_xcond_b_fc1': (0.0, 1.631),
     'L1_xcond_b_fc2': (0.0, 0.505)}
    factors = {'L0_xcond_g1_w': 8.0,
     'L0_xcond_g2_w': 4.376,
     'L0_xcond_b2_w': 4.579,
     'L0_xcond_sa_wq': 8.0,
     'L0_xcond_ca_wq': 8.0,
     'L1_xcond_W_ada': 4.316,
     'L1_xcond_W_qkv': 4.102,
     'L1_xcond_W_ctx': 8.0,
     'L1_xcond_W_q': 8.0,
     'L1_xcond_W_k': 8.0,
     'L1_xcond_W_v': 7.775,
     'L1_xcond_W_out': 7.843,
     'L1_xcond_W_fc1': 3.449}
    for name, (base, spread) in spreads.items():
        noise = np.random.default_rng([zlib.crc32(name.encode()), seed]).standard_normal(out[name].shape)
        drawn = base * np.exp(spread * noise) if base else spread * noise
        out[name] = jnp.asarray(drawn.astype(out[name].dtype))
    for name, factor in factors.items():
        out[name] = (out[name] * factor).astype(out[name].dtype)
    return out
```

```python
from contextlib import ExitStack
from functools import partial

import numpy as np

import concourse.bass as bass
from concourse import mybir

F32 = mybir.dt.float32
ALU = mybir.AluOpType
ACT = mybir.ActivationFunctionType
AX = mybir.AxisListType

P = 128
B = 8
HALF = B // 2
BANK = HALF * P
DC = 96
H = 16
DH0 = 64
DH1 = 8
STEPS = H // 2
FF = 4
VW = 32
EPS0, EPS1 = 1e-5, 1e-6

VECS = ["ln1_w", "ln1_b", "g1_b", "b1_b", "ln2_w", "ln2_b", "g2_b", "b2_b", "lnc_w", "lnc_b", "b_q", "b_k", "b_v",
        "b_ctx"] + [f"ada{j}" for j in range(6)] + [f"ffb{c}" for c in range(FF)] + [f"fcb{c}" for c in range(FF)]
COL = {name: i for i, name in enumerate(VECS)}
ROWS = {name: i for i, name in enumerate(["sa_bo", "ca_bo", "ff_b2", "b_proj", "b_out", "b_fc2"])}
SQ = {name: i for i, name in enumerate(["q", "k", "v", "proj", "cq", "ck", "cv", "out", "ctx"])}
IDENT, COS, SIN, MASK = 0, P, 2 * P, 3 * P
NCONST = 3 * P + H


def build(nc, x_in, ctx_in, ctxT_in, condT_in, wqkv_in, wo_in, wmod_in, wsq_in, wff_in, vec_in, row_in, const_in, out):
    es = ExitStack()
    with es:
        def sb(name, shape):
            return es.enter_context(nc.sbuf_tensor(name, shape, F32))

        def sem(name):
            return es.enter_context(nc.semaphore(name))

        x = sb("x", [P, B, P])
        xn = sb("xn", [P, B, P])
        hT = sb("hT", [P, B * P])
        ctx = sb("ctx", [P, B, DC])
        ctxT = sb("ctxT", [DC, B * P])
        ctxnT = sb("ctxnT", [DC, B * P])
        ctx1T = sb("ctx1T", [P, B * P])
        const = sb("const", [P, NCONST])
        vec = sb("vec", [P, len(VECS)])
        rows = sb("rows", [1, len(ROWS) * P])
        ones = sb("ones", [1, P])
        wmod = sb("wmod", [P, 10 * P])
        wsq = sb("wsq", [P, len(SQ) * P])
        wff = sb("wff", [P, 4 * FF * P])
        condT = sb("condT", [P, B])
        silu = sb("silu", [P, 4, B])
        mod = sb("mod", [P, 10, B])
        tmp = sb("tmp", [P, 4, B])
        bq_scaled = sb("bq_scaled", [P, 1])
        st = sb("st", [P, B, 6])
        mv = sb("mv", [P, B, 2])
        vare = sb("vare", [P, B])
        neg_half = sb("neg_half", [P, B])
        rstd = sb("rstd", [P, B])
        wqkv = sb("wqkv", [P, 2, 3 * P])
        wo = sb("wo", [P, 2, P])
        raw = sb("raw", [P, 4, BANK])
        swp = sb("swp", [P, 4, BANK])
        qk = sb("qk", [P, 2, 4, BANK])
        v0 = sb("v0", [P, 2, B * P])
        prob = sb("prob", [P, 4, BANK])
        probT = sb("probT", [P, 4, BANK])
        nmax = sb("nmax", [P, 4 * HALF])
        zsum = sb("zsum", [P, 4 * HALF])
        rz = sb("rz", [P, 4 * HALF])
        oT = sb("oT", [P, B * P])
        q1 = sb("q1", [P, B * P])
        k1 = sb("k1", [P, 2, B * P])
        v1 = sb("v1", [P, 2, B, P])
        km = sb("km", [P, 2, 2, B * P])
        vst = sb("vst", [P, 2, B, 2, VW])
        oS = sb("oS", [P, BANK])
        rzo = sb("rzo", [P, 2 * B])
        oN = sb("oN", [P, B, P])
        gT = sb("gT", [P, FF, B * P])

        bank = [es.enter_context(nc.psum_tensor(f"bank{i}", [P, BANK], F32)) for i in range(8)]
        ident = const[:, IDENT:IDENT + P]
        cos = const[:, COS:COS + P].unsqueeze(1).broadcast_to([P, HALF, P])
        sin = const[:, SIN:SIN + P].unsqueeze(1).broadcast_to([P, HALF, P])

        def four(ap):
            return ap.rearrange("p (u t) -> p u t", u=HALF)

        ld_x, ld_ctx, ld_ctxT, ld_small, ld_mod, ld_sq, ld_ff = (
            sem(f"ld_{s}") for s in ("x", "ctx", "ctxT", "small", "mod", "sq", "ff"))
        ld_wqkv = [sem(f"ld_wqkv{p}") for p in range(2)]
        ld_wo = [sem(f"ld_wo{p}") for p in range(2)]
        dve_link = sem("dve_link")
        presets = sem("presets")
        exp_c, silu_done, mod_ps, mod_done = sem("exp_c"), sem("silu_done"), sem("mod_ps"), sem("mod_done")
        ln_mv, ln_rstd, ln_xn, ln_T, ln_hT = (sem(f"ln_{s}") for s in ("mv", "rstd", "xn", "T", "hT"))
        scores, rowmax, exps, recips, norms, probs_T, probs_Tc, pv, o_copied = (
            sem(s) for s in ("scores", "rowmax", "exps", "recips", "norms", "probs_T", "probs_Tc", "pv", "o_copied"))
        fills, fills_out, rope_cos, rope_sin, roped, wo_done = (
            sem(s) for s in ("fills", "fills_out", "rope_cos", "rope_sin", "roped", "wo_done"))
        swapped = [sem(f"swapped{f}") for f in range(4)]
        acc_done = sem("acc_done")
        x_done = sem("x_done")
        a_scores, a_rowmax, a_exps, a_T, a_pv, a_ev, a_back, a_rzo, a_norm, a_km, a_vst = (
            sem(f"a_{s}") for s in ("scores", "rowmax", "exps", "T", "pv", "ev", "back", "rzo", "norm", "km", "vst"))
        a_Tc = [sem("a_Tc_even"), sem("a_Tc_odd")]
        pre, pre_out = sem("pre"), sem("pre_out")
        post_T, post_oT = sem("post_T"), sem("post_oT")
        ffn_h, ffn_g = sem("ffn_h"), sem("ffn_g")
        stored = sem("stored")

        PRE0 = [("ctx1", 0), ("ctx1", 1), ("ck", 0), ("ck", 1), ("cv", 0), ("cv", 1)]
        PRE1 = [("q", 0), ("q", 1), ("k", 0), ("k", 1), ("v", 0), ("v", 1)]
        PRE2 = [("cq", 0), ("cq", 1)]
        PRE_ALL = PRE0 + PRE1 + PRE2
        PRE_BANKS = [0, 1, 4, 5]
        PRE_BASE = [0, len(PRE0), len(PRE0) + len(PRE1)]

        def head_pairs(eng, first, step):
            step(first, first % 2, True, False)
            with eng.Fori(0, (STEPS - 2) // 2) as r:
                for p in range(2):
                    step(r * 2 + (first + 1 + p), (first + 1 + p) % 2, False, False)
            step(first + STEPS - 1, (first + STEPS - 1) % 2, False, True)

        block = es.enter_context(nc.Block())

        @block.sync
        def _(sp):
            sp.dma_start(x[:, :, :], x_in.rearrange("b t d -> t b d")).then_inc(ld_x, 16)
            sp.dma_start(const[:, :], const_in).then_inc(ld_small, 16)
            sp.dma_start(vec[:, :], vec_in).then_inc(ld_small, 16)
            sp.dma_start(condT[:, :], condT_in).then_inc(ld_small, 16)
            sp.dma_start(rows[:, :], row_in).then_inc(ld_small, 16)

            def swap(m, f):
                sp.wait_ge(fills_out, m * 6 + (f + 1))
                for e in range(2):
                    sp.dma_start(swp[e:P:2, f, :], raw[1 - e:P:2, f, :]).then_inc(swapped[f], 16)

            def load_wqkv(n, p):
                sp.wait_ge(fills, n * 6 + 6)
                sp.dma_start(wqkv[:, p, :], wqkv_in[bass.ds(n + 2, 1), :, :].rearrange("o p c -> p (o c)")).then_inc(
                    ld_wqkv[p], 16)

            def load_wo(n, p):
                sp.wait_ge(wo_done, n * 2)
                sp.dma_start(wo[:, 1 - p, :], wo_in[bass.ds(n + 1, 1), :, :].rearrange("o p c -> p (o c)")).then_inc(
                    ld_wo[1 - p], 16)

            def l0_step(n, p, is_first, is_last, a):
                if not (a == 1 and is_last):
                    load_wqkv(n, p)
                if not is_last:
                    for f in range(4):
                        swap(n + 1, f)
                if not (a == 0 and is_first) and not (a == 1 and is_last):
                    load_wo(n, p)

            for a in range(2):
                for f in range(4):
                    swap(STEPS * a, f)
                head_pairs(sp, STEPS * a, partial(l0_step, a=a))
            for half in range(2):
                b0 = HALF * half
                sp.wait_ge(x_done, half + 1)
                sp.dma_start(out[b0:b0 + HALF, :, :].rearrange("b t d -> t b d"), x[:, b0:b0 + HALF, :]).then_inc(
                    stored, 16)
            sp.wait_ge(stored, 32)

        @block.gpsimd
        def _(pool):
            pool.dma_start(ctx[:, :, :], ctx_in.rearrange("b t d -> t b d")).then_inc(ld_ctx, 16)
            pool.dma_start(ctxT[:, :], ctxT_in).then_inc(ld_ctxT, 16)
            pool.dma_start(wsq[:, :], wsq_in).then_inc(ld_sq, 16)
            for p in range(2):
                pool.memset(vst[:, p, :, :, DH1 + 1:VW], 0.0).then_inc(presets, 1)
                pool.memset(vst[:, p, :, :, DH1:DH1 + 1], 1.0).then_inc(presets, 1)

            def inv_std(k):
                for half in range(2):
                    cols = slice(HALF * half, HALF * (half + 1))
                    pool.wait_ge(ln_mv, 2 * k + half + 1)
                    nc.gpsimd.tensor_tensor(rstd[:, cols], vare[:, cols], neg_half[:, cols], ALU.pow).then_inc(ln_rstd, 1)

            def rope_sine(m, f):
                pool.wait_ge(swapped[f], m * 32 + 32)
                nc.gpsimd.tensor_tensor(four(swp[:, f, :]), four(swp[:, f, :]), sin, ALU.mult).then_inc(rope_sin, 1)

            def l0_step(n, p, is_first, is_last):
                if not is_last:
                    for f in range(4):
                        rope_sine(n + 1, f)

            def stage_values(m, p, a):
                if isinstance(m, int) and m == 0:
                    pool.wait_ge(presets, 5)
                else:
                    pool.wait_ge(a_pv, m * 4 - 4)
                src = v1[:, a, :, bass.ds(m * (2 * DH1) - a * P, 2 * DH1)].rearrange("p b (h d) -> p b h d", h=2)
                nc.gpsimd.tensor_copy(vst[:, p, :, :, 0:DH1], src).then_inc(a_vst, 1)

            def l1_step(n, p, is_first, is_last, a):
                if not is_last:
                    stage_values(n + 1, 1 - p, a)

            inv_std(0)
            for a in range(2):
                inv_std(1 + a)
                pool.wait_ge(ld_small, 64)
                for f in range(4):
                    rope_sine(STEPS * a, f)
                head_pairs(pool, STEPS * a, l0_step)
            inv_std(3)
            for a in range(2):
                inv_std(4 + a)
                pool.wait_ge(pre_out, len(PRE_ALL) - len(PRE2) if a == 0 else len(PRE_ALL))
                stage_values(STEPS * a, 0, a)
                head_pairs(pool, STEPS * a, partial(l1_step, a=a))
            inv_std(6)

        @block.scalar
        def _(act):
            act.dma_start(wmod[:, :], wmod_in).then_inc(ld_mod, 16)
            act.dma_start(wqkv[:, 0, :], wqkv_in[0, :, :]).then_inc(ld_wqkv[0], 16)
            act.dma_start(wo[:, 0, :], wo_in[0, :, :]).then_inc(ld_wo[0], 16)
            act.dma_start(wqkv[:, 1, :], wqkv_in[1, :, :]).then_inc(ld_wqkv[1], 16)
            act.dma_start(wo[:, 1, :], wo_in[1, :, :]).then_inc(ld_wo[1], 16)
            act.dma_start(wff[:, :], wff_in).then_inc(ld_ff, 16)
            act.wait_ge(ld_small, 64)
            nc.scalar.activation(silu[:, 0, :], condT[:, :], ACT.Exp, scale=-1.0).then_inc(exp_c, 1)

            def ln_scale_shift(k):
                for half in range(2):
                    act.wait_ge(ln_T, 2 * k + half + 1)
                    if k == 0:
                        nc.scalar.activation(ctxnT[:, half * BANK:(half + 1) * BANK], bank[2 + half][0:DC, :],
                                             ACT.Identity, bias=vec[0:DC, COL["lnc_b"]:COL["lnc_b"] + 1],
                                             scale=vec[0:DC, COL["lnc_w"]:COL["lnc_w"] + 1]).then_inc(ln_hT, 1)
                        continue
                    if k == 1 and half == 0:
                        act.wait_ge(mod_done, 1)
                    j = {1: 0, 2: 0, 3: 2, 4: 4, 5: 6, 6: 8}[k]
                    for u in range(HALF):
                        b = HALF * half + u
                        last = nc.scalar.activation(hT[:, b * P:(b + 1) * P], bank[2 + half][:, u * P:(u + 1) * P],
                                                    ACT.Identity, bias=mod[:, j + 1, b:b + 1], scale=mod[:, j, b:b + 1])
                    last.then_inc(ln_hT, 1)

            def evacuate_fill(m, f, mp, first=False):
                act.wait_ge(fills, m * 6 + (f + 1))
                if f < 4:
                    if not first:
                        act.wait_ge(roped, m * 4 + (f - 3))
                    ins = nc.scalar.activation(raw[:, f, :], bank[5][:, :], ACT.Copy,
                                               scale=DH0 ** -0.5 if f < 2 else 1.0)
                else:
                    ins = nc.scalar.activation(v0[:, mp, (f - 4) * BANK:(f - 3) * BANK], bank[5][:, :], ACT.Copy)
                ins.then_inc(fills_out, 1)

            def exp0(n, g):
                act.wait_ge(rowmax, n * 4 + (g + 1))
                for u in range(HALF):
                    c = g * HALF + u
                    last = nc.scalar.activation(prob[:, g, u * P:(u + 1) * P], bank[g % 2][:, u * P:(u + 1) * P],
                                                ACT.Exp, bias=nmax[:, c:c + 1], accum_out=zsum[:, c:c + 1])
                last.then_inc(exps, 1)

            def evacuate_o(n, half):
                act.wait_ge(pv, n * 2 + (half + 1))
                nc.scalar.activation(oT[:, half * BANK:(half + 1) * BANK], bank[4][:, :], ACT.Copy).then_inc(o_copied, 1)

            def l0_step(n, p, is_first, is_last):
                fill = not is_last
                exp0(n, 0)
                if fill:
                    evacuate_fill(n + 1, 0, 1 - p)
                exp0(n, 1)
                if fill:
                    evacuate_fill(n + 1, 1, 1 - p)
                    evacuate_fill(n + 1, 2, 1 - p)
                exp0(n, 2)
                if fill:
                    evacuate_fill(n + 1, 3, 1 - p)
                exp0(n, 3)
                evacuate_o(n, 0)
                if fill:
                    evacuate_fill(n + 1, 4, 1 - p)
                    evacuate_fill(n + 1, 5, 1 - p)
                evacuate_o(n, 1)

            def pre_evacuate(j):
                what, half = PRE_ALL[j]
                act.wait_ge(pre, j + 1)
                src = bank[PRE_BANKS[j % 4]][:, :]
                cols = slice(half * BANK, (half + 1) * BANK)
                if what == "ctx1":
                    ins = nc.scalar.activation(ctx1T[:, cols], src, ACT.Identity, bias=vec[:, COL["b_ctx"]:COL["b_ctx"] + 1])
                elif what == "q":
                    ins = nc.scalar.activation(q1[:, cols], src, ACT.Identity, bias=bq_scaled[:, :], scale=DH1 ** -0.5)
                elif what == "cq":
                    ins = nc.scalar.activation(q1[:, cols], src, ACT.Copy, scale=DH1 ** -0.5)
                elif what == "k":
                    ins = nc.scalar.activation(k1[:, 0, cols], src, ACT.Identity, bias=vec[:, COL["b_k"]:COL["b_k"] + 1])
                elif what == "ck":
                    ins = nc.scalar.activation(k1[:, 1, cols], src, ACT.Copy)
                else:
                    a = 0 if what == "v" else 1
                    ins = nc.scalar.activation(v1[:, a, HALF * half:HALF * (half + 1), :], four(src), ACT.Copy)
                ins.then_inc(pre_out, 1)

            def gelu(k, func, bias):
                base = 0 if k == 3 else 2 * FF
                for j in range(2 * FF):
                    c, half = j % FF, j // FF
                    act.wait_ge(ffn_h, base + j + 1)
                    col = COL[f"{bias}{c}"]
                    nc.scalar.activation(gT[:, c, half * BANK:(half + 1) * BANK], bank[PRE_BANKS[j % 4]][:, :], func,
                                         bias=vec[:, col:col + 1]).then_inc(ffn_g, 1)

            def exp1(n, g):
                act.wait_ge(a_rowmax, n * 4 + (g + 1))
                for u in range(HALF):
                    c = g * HALF + u
                    last = nc.scalar.activation(prob[:, g, u * P:(u + 1) * P], bank[g][:, u * P:(u + 1) * P],
                                                ACT.Exp, bias=nmax[:, c:c + 1])
                last.then_inc(a_exps, 1)

            def copy_T(n, g):
                act.wait_ge(a_T, n * 4 + (g + 1))
                nc.scalar.activation(probT[:, g, :], bank[4 + g % 2][:, :], ACT.Copy).then_inc(a_Tc[1], 1)

            def evacuate_o1(n):
                act.wait_ge(a_pv, n * 4 + 4)
                nc.scalar.activation(oS[:, :], bank[6][:, :], ACT.Copy).then_inc(a_ev, 1)

            def l1_step(n, p, is_first, is_last, a):
                exp1(n, 0)
                if not is_first:
                    copy_T(n - 1, 3)
                    evacuate_o1(n - 1)
                exp1(n, 1)
                exp1(n, 2)
                copy_T(n, 1)
                exp1(n, 3)
                if is_last:
                    copy_T(n, 3)
                    evacuate_o1(n)

            def evacuate_post(a):
                for half in range(2):
                    act.wait_ge(post_T, 2 * a + half + 1)
                    dst, src = oT[:, half * BANK:(half + 1) * BANK], bank[4 + half][:, :]
                    if a == 0:
                        ins = nc.scalar.activation(dst, src, ACT.Identity, bias=vec[:, COL["b_v"]:COL["b_v"] + 1])
                    else:
                        ins = nc.scalar.activation(dst, src, ACT.Copy)
                    ins.then_inc(post_oT, 1)

            ln_scale_shift(0)
            for j in range(len(PRE0)):
                pre_evacuate(j)
            for a in range(2):
                ln_scale_shift(1 + a)
                for f in range(6):
                    evacuate_fill(STEPS * a, f, 0, first=(a == 0))
                head_pairs(act, STEPS * a, l0_step)
            ln_scale_shift(3)
            gelu(3, ACT.Gelu, "ffb")
            for a in range(2):
                ln_scale_shift(4 + a)
                for j in range(PRE_BASE[1 + a], PRE_BASE[1 + a] + len([PRE1, PRE2][a])):
                    pre_evacuate(j)
                head_pairs(act, STEPS * a, partial(l1_step, a=a))
                evacuate_post(a)
            ln_scale_shift(6)
            gelu(6, ACT.Gelu_apprx_tanh, "fcb")

        @block.vector
        def _(dve):
            links = [0]

            def link(ins):
                links[0] += 1
                ins.then_inc(dve_link, 1)
                dve.wait_ge(dve_link, links[0])

            nc.vector.memset(ones[:, :], 1.0).then_inc(presets, 1)
            nc.vector.memset(neg_half[:, :], -0.5)

            def ln_stats(k, src, half):
                for b in range(HALF * half, HALF * (half + 1)):
                    last = nc.vector.bn_stats(st[:, b, :], src[:, b, :])
                link(last)
                for b in range(HALF * half, HALF * (half + 1)):
                    last = nc.vector.bn_aggr(mv[:, b, :], st[:, b, :])
                link(last)
                cols = slice(HALF * half, HALF * (half + 1))
                nc.vector.tensor_scalar(vare[:, cols], mv[:, cols, 1], EPS0 if k < 4 else EPS1, None, ALU.add).then_inc(
                    ln_mv, 1)

            def ln_normalise(k, src, width):
                if k:
                    dve.wait_ge(ln_T, 2 * k)
                for half in range(2):
                    dve.wait_ge(ln_rstd, 2 * k + half + 1)
                    for b in range(HALF * half, HALF * (half + 1)):
                        last = nc.vector.tensor_scalar(xn[:, b, 0:width], src[:, b, :], mv[:, b, 0:1],
                                                       rstd[:, b:b + 1], ALU.subtract, ALU.mult)
                    last.then_inc(ln_xn, 1)

            def residual_and_norm(k, sublayer):
                for half in range(2):
                    if sublayer is not None:
                        xs = x[:, HALF * half:HALF * (half + 1), :]
                        if sublayer < 2:
                            dve.wait_ge(wo_done, 2 * STEPS * (sublayer + 1) - 1 + half)
                        else:
                            dve.wait_ge(acc_done, 2 * (sublayer - 2) + half + 1)
                        link(nc.vector.tensor_tensor(xs, xs, four(bank[6 + half][:, :]), ALU.add))
                    ln_stats(k, x, half)
                ln_normalise(k, x, P)

            def vcol(name, rows_=P):
                return vec[0:rows_, COL[name]:COL[name] + 1]

            def modulation():
                dve.wait_ge(exp_c, 1)
                link(nc.vector.tensor_scalar(silu[:, 1, :], silu[:, 0, :], 1.0, None, ALU.add))
                link(nc.vector.reciprocal(silu[:, 2, :], silu[:, 1, :]))
                nc.vector.tensor_tensor(silu[:, 3, :], silu[:, 2, :], condT[:, :], ALU.mult).then_inc(silu_done, 1)
                dve.wait_ge(mod_ps, 1)
                ps = bank[0][:, 0:10 * B].rearrange("p (j b) -> p j b", j=10)
                for i, ln in enumerate(("1", "2")):
                    nc.vector.tensor_scalar(tmp[:, 2 * i, :], ps[:, 2 * i, :], vcol(f"g{ln}_b"), 1.0, ALU.add, ALU.add)
                    link(nc.vector.tensor_scalar(tmp[:, 2 * i + 1, :], ps[:, 2 * i + 1, :], vcol(f"b{ln}_b"), None, ALU.add))
                    nc.vector.tensor_scalar(mod[:, 2 * i, :], tmp[:, 2 * i, :], vcol(f"ln{ln}_w"), None, ALU.mult)
                    nc.vector.scalar_tensor_tensor(mod[:, 2 * i + 1, :], tmp[:, 2 * i, :], vcol(f"ln{ln}_b"),
                                                   tmp[:, 2 * i + 1, :], ALU.mult, ALU.add)
                nc.vector.tensor_scalar(bq_scaled[:, :], vcol("b_q"), DH1 ** -0.5, None, ALU.mult)
                for i in range(3):
                    shift, scale = 2 * i, 2 * i + 1
                    nc.vector.tensor_scalar(mod[:, 4 + 2 * i, :], ps[:, 4 + scale, :], vcol(f"ada{scale}"), 1.0,
                                            ALU.add, ALU.add)
                    last = nc.vector.tensor_scalar(mod[:, 5 + 2 * i, :], ps[:, 4 + shift, :], vcol(f"ada{shift}"), None,
                                                   ALU.add)
                last.then_inc(mod_done, 1)

            def row_max(n, g):
                dve.wait_ge(scores, n * 4 + (g + 1))
                nc.vector.tensor_reduce(nmax[:, g * HALF:(g + 1) * HALF], four(bank[g % 2][:, :]), AX.X, ALU.max,
                                        negate=True).then_inc(rowmax, 1)

            def normalise(n, g):
                dve.wait_ge(exps, n * 4 + (g + 1))
                cols = slice(g * HALF, (g + 1) * HALF)
                nc.vector.reciprocal(rz[:, cols], zsum[:, cols]).then_inc(recips, 1)
                dve.wait_ge(recips, n * 4 + (g + 1))
                nc.vector.tensor_tensor(four(prob[:, g, :]), four(prob[:, g, :]),
                                        rz[:, cols].unsqueeze(2).broadcast_to([P, HALF, P]), ALU.mult).then_inc(norms, 1)

            def copy_T0(n, g):
                dve.wait_ge(probs_T, n * 4 + (g + 1))
                nc.vector.tensor_copy(probT[:, g, :], bank[2 + g % 2][:, :]).then_inc(probs_Tc, 1)

            def rope_cosine(m, f, mp):
                dve.wait_ge(fills_out, m * 6 + (f + 1))
                nc.vector.tensor_tensor(four(qk[:, mp, f, :]), four(raw[:, f, :]), cos, ALU.mult).then_inc(rope_cos, 1)

            def rope_sum(m, f, mp):
                dve.wait_ge(rope_sin, m * 4 + (f + 1))
                dve.wait_ge(rope_cos, m * 4 + (f + 1))
                nc.vector.tensor_tensor(qk[:, mp, f, :], qk[:, mp, f, :], swp[:, f, :], ALU.add).then_inc(roped, 1)

            def l0_step(n, p, is_first, is_last):
                fill = not is_last
                row_max(n, 0)
                row_max(n, 1)
                normalise(n, 0)
                if fill:
                    rope_cosine(n + 1, 0, 1 - p)
                copy_T0(n, 0)
                normalise(n, 1)
                if fill:
                    rope_cosine(n + 1, 1, 1 - p)
                row_max(n, 2)
                copy_T0(n, 1)
                if fill:
                    rope_cosine(n + 1, 2, 1 - p)
                    rope_sum(n + 1, 0, 1 - p)
                normalise(n, 2)
                row_max(n, 3)
                if fill:
                    rope_cosine(n + 1, 3, 1 - p)
                    rope_sum(n + 1, 1, 1 - p)
                normalise(n, 3)
                copy_T0(n, 2)
                if fill:
                    rope_sum(n + 1, 2, 1 - p)
                copy_T0(n, 3)
                if fill:
                    rope_sum(n + 1, 3, 1 - p)

            def mask_keys(m, p, a):
                for hh in range(2):
                    nc.vector.tensor_scalar(km[:, p, hh, :], k1[:, a, :], const[:, bass.ds(m * 2 + (MASK + hh - a * H), 1)],
                                            None, ALU.mult).then_inc(a_km, 1)

            def row_max1(n, g):
                dve.wait_ge(a_scores, n * 4 + (g + 1))
                nc.vector.tensor_reduce(nmax[:, g * HALF:(g + 1) * HALF], four(bank[g][:, :]), AX.X, ALU.max,
                                        negate=True).then_inc(a_rowmax, 1)

            def copy_T1(n, g):
                dve.wait_ge(a_T, n * 4 + (g + 1))
                nc.vector.tensor_copy(probT[:, g, :], bank[4 + g % 2][:, :]).then_inc(a_Tc[0], 1)

            def divide(n, a):
                dve.wait_ge(a_back, n + 1)
                src = bank[7][:, :].rearrange("p (h b v) -> p h b v", h=2, b=B)
                nc.vector.reciprocal(rzo[:, :].rearrange("p (h b) -> p h b", h=2), src[:, :, :, DH1]).then_inc(a_rzo, 1)
                dve.wait_ge(a_rzo, n + 1)
                dst = oN[:, :, bass.ds(n * (2 * DH1) - a * P, 2 * DH1)].rearrange("p b (h d) -> p h b d", h=2)
                nc.vector.tensor_tensor(dst, src[:, :, :, 0:DH1], rzo[:, :].rearrange("p (h b) -> p h b", h=2).unsqueeze(3)
                                        .broadcast_to([P, 2, B, DH1]), ALU.mult).then_inc(a_norm, 1)

            def l1_step(n, p, is_first, is_last, a):
                row_max1(n, 0)
                row_max1(n, 1)
                if not is_last:
                    mask_keys(n + 1, 1 - p, a)
                row_max1(n, 2)
                copy_T1(n, 0)
                row_max1(n, 3)
                if not is_first:
                    divide(n - 1, a)
                copy_T1(n, 2)
                if is_last:
                    divide(n, a)

            dve.wait_ge(ld_ctx, 16)
            ln_stats(0, ctx, 0)
            ln_stats(0, ctx, 1)
            dve.wait_ge(ld_x, 16)
            dve.wait_ge(ld_small, 64)
            modulation()
            ln_normalise(0, ctx, DC)
            for a in range(2):
                residual_and_norm(1 + a, None if a == 0 else 0)
                for f in range(4):
                    rope_cosine(STEPS * a, f, 0)
                for f in range(4):
                    rope_sum(STEPS * a, f, 0)
                head_pairs(dve, STEPS * a, l0_step)
            residual_and_norm(3, 1)
            for a in range(2):
                residual_and_norm(4 + a, 2 + a)
                dve.wait_ge(pre_out, PRE_BASE[1] + len(PRE1) if a == 0 else len(PRE_ALL))
                mask_keys(STEPS * a, 0, a)
                head_pairs(dve, STEPS * a, partial(l1_step, a=a))
            residual_and_norm(6, 4)
            for half in range(2):
                xs = x[:, HALF * half:HALF * (half + 1), :]
                dve.wait_ge(acc_done, 2 * 3 + half + 1)
                nc.vector.tensor_tensor(xs, xs, four(bank[6 + half][:, :]), ALU.add).then_inc(x_done, 1)

        @block.tensor
        def _(pe):
            def mm(o, lhsT, rhs, start, stop):
                return nc.tensor.matmul(o, lhsT, rhs, start=start, stop=stop, skip_group_check=True)

            def bcols(b):
                return slice(b * P, (b + 1) * P)

            def transpose_norm(k, width):
                for half in range(2):
                    pe.wait_ge(ln_xn, 2 * k + half + 1)
                    if k:
                        pe.wait_ge(ln_hT, 2 * k + half - 1)
                    for u in range(HALF):
                        last = nc.tensor.transpose(bank[2 + half][0:width, bcols(u)],
                                                   xn[:, HALF * half + u, 0:width], ident)
                    last.then_inc(ln_T, 1)

            def seed(name):
                row = rows[:, ROWS[name] * P:(ROWS[name] + 1) * P]
                for half in range(2):
                    for u in range(HALF):
                        mm(bank[6 + half][:, bcols(u)], ones[:, :], row, start=(u == 0), stop=False)

            def fill(m, f, mp, src, width, k=None):
                if k is not None:
                    pe.wait_ge(ln_hT, 2 * k + f % 2 + 1)
                if f == 0:
                    pe.wait_ge(ld_wqkv[mp], m * 8 + (16 - 8 * mp))
                pe.wait_ge(fills_out, m * 6 + f)
                half = f % 2
                cols = slice(half * BANK, (half + 1) * BANK)
                if f < 2:
                    last = mm(bank[5][:, :], wqkv[:, mp, 0:P], hT[:, cols], True, True)
                elif f < 4:
                    last = mm(bank[5][:, :], wqkv[0:width, mp, P:2 * P], src[:, cols], True, True)
                else:
                    for u in range(HALF):
                        last = mm(bank[5][:, bcols(u)], src[:, bcols(HALF * half + u)], wqkv[0:width, mp, 2 * P:3 * P],
                                  True, True)
                last.then_inc(fills, 1)

            def score(n, p, g, is_first):
                hh, half = g % 2, g // 2
                pe.wait_ge(roped, n * 4 + 3 + half)
                if g >= 2 or not is_first:
                    pe.wait_ge(exps, n * 4 + (g - 1))
                lanes = slice(DH0 * hh, DH0 * (hh + 1))
                for u in range(HALF):
                    last = mm(bank[g % 2][:, bcols(u)], qk[lanes, p, half, bcols(u)], qk[lanes, p, 2 + half, bcols(u)],
                              True, True)
                last.then_inc(scores, 1)

            def transpose_probs(n, g, is_first):
                pe.wait_ge(norms, n * 4 + (g + 1))
                if g >= 2 or not is_first:
                    pe.wait_ge(probs_Tc, n * 4 + (g - 1))
                for u in range(HALF):
                    last = nc.tensor.transpose(bank[2 + g % 2][:, bcols(u)], prob[:, g, bcols(u)], ident)
                last.then_inc(probs_T, 1)

            def prob_values(n, p, half, is_first):
                pe.wait_ge(probs_Tc, n * 4 + (2 * half + 2))
                pe.wait_ge(fills_out, n * 6 + 6)
                if half or not is_first:
                    pe.wait_ge(o_copied, n * 2 + half)
                for u in range(HALF):
                    for hh in range(2):
                        b = HALF * half + u
                        last = mm(bank[4][DH0 * hh:DH0 * (hh + 1), bcols(u)],
                                  v0[:, p, b * P + DH0 * hh:b * P + DH0 * (hh + 1)], probT[:, 2 * half + hh, bcols(u)],
                                  True, True)
                last.then_inc(pv, 1)

            def project_out(n, p, half):
                pe.wait_ge(o_copied, n * 2 + (half + 1))
                if half == 0:
                    pe.wait_ge(ld_wo[p], n * 8 + (16 - 8 * p))
                for u in range(HALF):
                    last = mm(bank[6 + half][:, bcols(u)], oT[:, bcols(HALF * half + u)], wo[:, p, :], False, False)
                last.then_inc(wo_done, 1)

            def l0_step(n, p, is_first, is_last, src, width):
                def fills_of_next(f):
                    if not is_last:
                        fill(n + 1, f, 1 - p, src, width)

                score(n, p, 0, is_first)
                score(n, p, 1, is_first)
                fills_of_next(0)
                if not is_first:
                    project_out(n - 1, 1 - p, 0)
                fills_of_next(1)
                transpose_probs(n, 0, is_first)
                score(n, p, 2, is_first)
                fills_of_next(2)
                transpose_probs(n, 1, is_first)
                fills_of_next(3)
                score(n, p, 3, is_first)
                if not is_first:
                    project_out(n - 1, 1 - p, 1)
                prob_values(n, p, 0, is_first)
                transpose_probs(n, 2, is_first)
                fills_of_next(4)
                transpose_probs(n, 3, is_first)
                fills_of_next(5)
                prob_values(n, p, 1, is_first)

            def pre_fill(j):
                what, half = PRE_ALL[j]
                if j >= 4:
                    pe.wait_ge(pre_out, j - 3)
                if what in ("ck", "cv"):
                    pe.wait_ge(pre_out, half + 1 if what == "ck" else 2)
                if what in ("q", "k", "v"):
                    pe.wait_ge(ln_hT, 8 + half + 1)
                if what == "cq":
                    pe.wait_ge(ln_hT, 10 + half + 1)
                ps = bank[PRE_BANKS[j % 4]]
                w = wsq[0:DC if what == "ctx1" else P, SQ["ctx" if what == "ctx1" else what] * P:][:, 0:P]
                src = {"ctx1": ctxT, "ck": ctx1T, "cv": ctx1T}.get(what, hT)
                if what in ("v", "cv"):
                    for u in range(HALF):
                        last = mm(ps[:, bcols(u)], src[:, bcols(HALF * half + u)], w, True, True)
                else:
                    last = mm(ps[:, :], w, src[:, half * BANK:(half + 1) * BANK], True, True)
                last.then_inc(pre, 1)

            def score1(n, p, g, lead):
                hh, half = g // 2, g % 2
                pe.wait_ge(a_km, n * 2 + (hh + 1))
                if not lead:
                    pe.wait_ge(a_exps, n * 4 + (g - 3))
                for u in range(HALF):
                    b = HALF * half + u
                    last = mm(bank[g][:, bcols(u)], q1[:, bcols(b)], km[:, p, hh, bcols(b)], True, True)
                last.then_inc(a_scores, 1)

            def transpose1(n, g, lead):
                pe.wait_ge(a_exps, n * 4 + (g + 1))
                if g >= 2:
                    pe.wait_ge(a_Tc[g % 2], n * 2 + (g // 2))
                elif not lead:
                    pe.wait_ge(a_Tc[g % 2], n * 2)
                for u in range(HALF):
                    last = nc.tensor.transpose(bank[4 + g % 2][:, bcols(u)], prob[:, g, bcols(u)], ident)
                last.then_inc(a_T, 1)

            def prob_values1(n, p, g, lead):
                hh, half = g // 2, g % 2
                pe.wait_ge(a_Tc[g % 2], n * 2 + (g // 2 + 1))
                if g == 0:
                    pe.wait_ge(a_vst, n + 1)
                    if not lead:
                        pe.wait_ge(a_ev, n)
                for u in range(HALF):
                    last = mm(bank[6][VW * u:VW * (u + 1), bcols(g)], vst[:, p, HALF * half + u, hh, :],
                              probT[:, g, bcols(u)], True, True)
                last.then_inc(a_pv, 1)

            def turn_back(n, lead):
                pe.wait_ge(a_ev, n + 1)
                if not lead:
                    pe.wait_ge(a_norm, n)
                for g in range(4):
                    last = nc.tensor.transpose(bank[7][:, bcols(g)], oS[:, bcols(g)], ident)
                last.then_inc(a_back, 1)

            def l1_step(n, p, is_first, is_last, a):
                lead = is_first and a == 0
                if is_first:
                    for g in range(3):
                        score1(n, p, g, lead)
                score1(n, p, 3, lead)
                transpose1(n, 0, lead)
                if not is_first:
                    prob_values1(n - 1, 1 - p, 3, False)
                if not is_last:
                    score1(n + 1, 1 - p, 0, False)
                transpose1(n, 1, lead)
                prob_values1(n, p, 0, lead)
                if not is_last:
                    score1(n + 1, 1 - p, 1, False)
                transpose1(n, 2, lead)
                prob_values1(n, p, 1, lead)
                if not is_first:
                    turn_back(n - 1, False)
                if not is_last:
                    score1(n + 1, 1 - p, 2, False)
                transpose1(n, 3, lead)
                prob_values1(n, p, 2, lead)
                if is_last:
                    prob_values1(n, p, 3, lead)
                    turn_back(n, False)

            def project_out1(a):
                pe.wait_ge(a_norm, STEPS * (a + 1))
                for half in range(2):
                    for u in range(HALF):
                        last = nc.tensor.transpose(bank[4 + half][:, bcols(u)], oN[:, HALF * half + u, :], ident)
                    last.then_inc(post_T, 1)
                seed("b_proj" if a == 0 else "b_out")
                w = wsq[:, SQ["proj" if a == 0 else "out"] * P:][:, 0:P]
                for half in range(2):
                    pe.wait_ge(post_oT, 2 * a + half + 1)
                    for u in range(HALF):
                        last = mm(bank[6 + half][:, bcols(u)], oT[:, bcols(HALF * half + u)], w, False, False)
                    last.then_inc(acc_done, 1)

            def mlp(k):
                base = 0 if k == 3 else 2 * FF
                off = 0 if k == 3 else 2 * FF * P
                seed("ff_b2" if k == 3 else "b_fc2")

                def down(half):
                    pe.wait_ge(ffn_g, base + FF * (half + 1))
                    for u in range(HALF):
                        for c in range(FF):
                            last = mm(bank[6 + half][:, bcols(u)], gT[:, c, bcols(HALF * half + u)],
                                      wff[:, off + (FF + c) * P:off + (FF + c + 1) * P], False, False)
                    last.then_inc(acc_done, 1)

                for j in range(2 * FF):
                    c, half = j % FF, j // FF
                    if c == 0:
                        pe.wait_ge(ln_hT, 2 * k + half + 1)
                    if j >= 4:
                        pe.wait_ge(ffn_g, base + j - 3)
                    mm(bank[PRE_BANKS[j % 4]][:, :], wff[:, off + c * P:off + (c + 1) * P],
                       hT[:, half * BANK:(half + 1) * BANK], True, True).then_inc(ffn_h, 1)
                down(0)
                down(1)

            pe.wait_ge(ld_small, 64)
            pe.wait_ge(ld_mod, 16)
            pe.wait_ge(silu_done, 1)
            for j in range(10):
                last = mm(bank[0][:, j * B:(j + 1) * B], wmod[:, bcols(j)], condT[:, :] if j < 4 else silu[:, 3, :],
                          True, True)
            last.then_inc(mod_ps, 1)
            transpose_norm(0, DC)
            pe.wait_ge(ld_sq, 16)
            pe.wait_ge(ld_ctxT, 16)
            pe.wait_ge(mod_done, 1)
            for j in range(len(PRE0)):
                pre_fill(j)
            pe.wait_ge(presets, 5)
            pe.wait_ge(pre_out, len(PRE0))
            for a in range(2):
                transpose_norm(1 + a, P)
                seed("sa_bo" if a == 0 else "ca_bo")
                src, width = (hT, P) if a == 0 else (ctxnT, DC)
                for f in range(6):
                    fill(STEPS * a, f, 0, src, width, k=1 + a)
                head_pairs(pe, STEPS * a, partial(l0_step, src=src, width=width))
                n = STEPS * (a + 1) - 1
                for half in range(2):
                    project_out(n, 1, half)
            transpose_norm(3, P)
            pe.wait_ge(ld_ff, 16)
            mlp(3)
            for a in range(2):
                transpose_norm(4 + a, P)
                for j in range(PRE_BASE[1 + a], PRE_BASE[1 + a] + len([PRE1, PRE2][a])):
                    pre_fill(j)
                head_pairs(pe, STEPS * a, partial(l1_step, a=a))
                project_out1(a)
            transpose_norm(6, P)
            mlp(6)


def _packed(i):
    def pad(w):
        return np.concatenate([w, np.zeros((P - w.shape[0], *w.shape[1:]), w.dtype)], axis=0)

    wqkv = []
    for wq, wkv in (("sa_wq", "sa_wkv"), ("ca_wq", "ca_wkv")):
        q, kv = i["L0_xcond_" + wq], pad(i["L0_xcond_" + wkv])
        for s in range(STEPS):
            c = slice(P * s, P * (s + 1))
            wqkv.append(np.concatenate([q[:, c], kv[:, c], kv[:, H * DH0:][:, c]], axis=1))
    wqkv.append(np.zeros_like(wqkv[0]))
    wo = np.concatenate([i["L0_xcond_sa_wo"].reshape(STEPS, P, P), i["L0_xcond_ca_wo"].reshape(STEPS, P, P)], axis=0)
    wmod = np.concatenate([i["L0_xcond_g1_w"], i["L0_xcond_b1_w"], i["L0_xcond_g2_w"], i["L0_xcond_b2_w"],
                           i["L1_xcond_W_ada"]], axis=1)
    wsq = np.concatenate([i["L1_xcond_W_qkv"], i["L1_xcond_W_proj"], i["L1_xcond_W_q"], i["L1_xcond_W_k"],
                          i["L1_xcond_W_v"], i["L1_xcond_W_out"], pad(i["L1_xcond_W_ctx"])], axis=1)

    def down(w):
        return w.reshape(FF, P, P).transpose(1, 0, 2).reshape(P, FF * P)

    wff = np.concatenate([i["L0_xcond_ff_w1"], down(i["L0_xcond_ff_w2"]), i["L1_xcond_W_fc1"], down(i["L1_xcond_W_fc2"])],
                         axis=1)
    bqkv = i["L1_xcond_b_qkv"].reshape(3, P)
    vecs = [i["L0_xcond_" + n] for n in ("ln1_w", "ln1_b", "g1_b", "b1_b", "ln2_w", "ln2_b", "g2_b", "b2_b")]
    vecs += [pad(i["L0_xcond_ca_lnc_w"]), pad(i["L0_xcond_ca_lnc_b"]), bqkv[0], bqkv[1], bqkv[2], i["L1_xcond_b_ctx"]]
    vecs += list(i["L1_xcond_b_ada"].reshape(6, P)) + list(i["L0_xcond_ff_b1"].reshape(FF, P))
    vecs += list(i["L1_xcond_b_fc1"].reshape(FF, P))
    rows = np.concatenate([i["L0_xcond_sa_bo"], i["L0_xcond_ca_bo"], i["L0_xcond_ff_b2"], i["L1_xcond_b_proj"],
                           i["L1_xcond_b_out"], i["L1_xcond_b_fc2"]]).reshape(1, -1)
    chan = np.arange(P) % DH0
    inv = (np.float32(1.0) / np.float32(10000.0) ** (np.arange(0, DH0, 2, dtype=np.float32) / np.float32(DH0)))
    ang = (np.arange(P, dtype=np.float32)[:, None] * inv.astype(np.float32)[None, :]).astype(np.float32)
    cos, sin = np.cos(ang).T[chan // 2], np.sin(ang).T[chan // 2]
    sin = np.where(chan[:, None] % 2 == 0, -sin, sin)
    mask = (np.arange(P)[:, None] // DH1 == np.arange(H)[None, :])
    const = np.concatenate([np.eye(P), cos, sin, mask], axis=1).astype(np.float32)
    return {
        "x": i["x"], "ctx": i["ctx_768"], "ctxT": i["ctx_768"].reshape(B * P, DC).T, "condT": i["cond_1024"].T,
        "wqkv": np.stack(wqkv), "wo": wo, "wmod": wmod, "wsq": wsq, "wff": wff, "vec": np.stack(vecs, axis=1),
        "row": rows, "const": const,
    }


def kernel(**inputs):
    import concourse.bacc as bacc
    from concourse.bass_utils import run_bass_kernel_spmd

    nc = bacc.Bacc("TRN2", target_bir_lowering=False, num_devices=1)
    arrays, args = {}, []
    for name, a in _packed({k: np.asarray(v) for k, v in inputs.items()}).items():
        arrays[f"in_{name}"] = np.ascontiguousarray(a)
        args.append(nc.dram_tensor(f"in_{name}", a.shape, F32, kind="ExternalInput").ap())
    args.append(nc.dram_tensor("out_x", (B, P, P), F32, kind="ExternalOutput").ap())
    build(nc, *args)
    return run_bass_kernel_spmd(nc, [arrays], core_ids=[0]).results[0]["out_x"]
```

```python
from contextlib import ExitStack
from functools import partial

import numpy as np

import concourse.bass as bass
from concourse import mybir

F32 = mybir.dt.float32
BF16 = mybir.dt.bfloat16
ALU = mybir.AluOpType
ACT = mybir.ActivationFunctionType
AX = mybir.AxisListType

P = 128
B = 8
HALF = B // 2
BANK = HALF * P
DC = 96
H = 16
DH0 = 64
DH1 = 8
STEPS = H // 2
FF = 4
VW = 32
EPS0, EPS1 = 1e-5, 1e-6

VECS = ["g1_b", "b1_b", "g2_b", "b2_b", "ada1", "ada0", "ada3", "ada2", "ada5", "ada4", "ln1_w", "ln1_b", "ln2_w", "ln2_b",
        "lnc_w", "lnc_b", "b_q", "b_k", "b_v", "b_ctx"] + [f"ffb{c}" for c in range(FF)] + [f"fcb{c}" for c in range(FF)]
COL = {name: i for i, name in enumerate(VECS)}
ROWS = {name: i for i, name in enumerate(["sa_bo", "ca_bo", "ff_b2", "b_proj", "b_out", "b_fc2"])}
SQ = {name: i for i, name in enumerate(["q", "k", "v", "proj", "cq", "ck", "cv", "out", "ctx"])}
IDENT, COS, SIN, MASK = 0, P, 2 * P, 3 * P
COND = MASK + H
VEC = COND + B
NSMALL = VEC + len(VECS)
NMOD = 10

FILLS = ["q0", "k0", "q1", "k1", "v0", "v1"]


def build(nc, small_in, x_in, ctx_in, ctxT_in, wqkv_in, wo_in, wmod_in, wsq_in, wff_in, row_in, out):
    es = ExitStack()
    with es:
        def sb(name, shape, dt=F32):
            return es.enter_context(nc.sbuf_tensor(name, shape, dt))

        def sem(name):
            return es.enter_context(nc.semaphore(name))

        x = sb("x", [P, B, P])
        xn = sb("xn", [P, B, P])
        hT = sb("hT", [P, B * P])
        ctx = sb("ctx", [P, B, DC])
        ctxT = sb("ctxT", [DC, B * P])
        ctxnT = sb("ctxnT", [DC, B * P])
        ctx1T = sb("ctx1T", [P, B * P])
        small = sb("small", [P, NSMALL])
        rows = sb("rows", [len(ROWS), P])
        rest = sb("rest", [len(ROWS), P])
        parts = sb("parts", [len(ROWS), 3, P], BF16)
        parts_row = sb("parts_row", [3, len(ROWS) * P], BF16)
        ones = sb("ones", [3, P], BF16)
        wmod = sb("wmod", [P, 10 * P])
        wsq = sb("wsq", [P, len(SQ) * P])
        wff = sb("wff", [P, 4 * FF * P])
        silu = sb("silu", [P, 4, B])
        primer = sb("primer", [P, 1])
        mod = sb("mod", [P, NMOD, B])
        bq_scaled = sb("bq_scaled", [P, 1])
        st = sb("st", [P, 2, B, 6])
        mv = sb("mv", [P, 2, B, 2])
        vare = sb("vare", [P, 2, B])
        neg_half = sb("neg_half", [P, B])
        rstd = sb("rstd", [P, 2, B])
        wqkv = sb("wqkv", [P, 2, 3 * P])
        wo = sb("wo", [P, 2, P])
        raw = sb("raw", [P, 4, BANK])
        swp = sb("swp", [P, 4, BANK])
        qk = sb("qk", [P, 2, 4, BANK])
        v0 = sb("v0", [P, 2, B * P])
        prob = sb("prob", [P, 4, BANK])
        probT = sb("probT", [P, 4, BANK])
        nmax = sb("nmax", [P, 4 * HALF])
        zsum = sb("zsum", [P, 4 * HALF])
        rz = sb("rz", [P, 4 * HALF])
        oT = sb("oT", [P, B * P])
        q1 = sb("q1", [P, B * P])
        k1 = sb("k1", [P, 2, B * P])
        v1 = sb("v1", [P, 2, B, P])
        km = sb("km", [P, 2, 2, B * P])
        vst = sb("vst", [P, 2, B, 2, VW])
        oS = sb("oS", [P, BANK])
        rzo = sb("rzo", [P, 2 * B])
        oN = sb("oN", [P, B, P])
        gT = sb("gT", [P, FF, B * P])

        bank = [es.enter_context(nc.psum_tensor(f"bank{i}", [P, BANK], F32)) for i in range(8)]
        ident = small[:, IDENT:IDENT + P]
        condT = small[:, COND:COND + B]
        cos = small[:, COS:COS + P].unsqueeze(1).broadcast_to([P, HALF, P])
        sin = small[:, SIN:SIN + P].unsqueeze(1).broadcast_to([P, HALF, P])

        def vcol(name, n=P):
            return small[0:n, VEC + COL[name]:VEC + COL[name] + 1]

        def four(ap):
            return ap.rearrange("p (u t) -> p u t", u=HALF)

        def by_half(tile):
            return tile[:, :].rearrange("p (h f c) -> p h f c", h=2, f=2)

        ld_x = [sem(f"ld_x{half}") for half in range(2)]
        ld_ctx, ld_ctxT, ld_small, ld_rows, ld_mod, ld_sq, ld_ff = (
            sem(f"ld_{s}") for s in ("ctx", "ctxT", "small", "rows", "mod", "sq", "ff"))
        ld_wqkv = [sem(f"ld_wqkv{p}") for p in range(2)]
        ld_wo = [sem(f"ld_wo{p}") for p in range(2)]
        dve_link = sem("dve_link")
        presets = sem("presets")
        row_part = sem("row_part")
        row_moved = sem("row_moved")
        exp_c, silu_done, mod_ps, mod_done = sem("exp_c"), sem("silu_done"), sem("mod_ps"), sem("mod_done")
        ctx_mv, ctx_rstd, ctx_n, ctx_T, ctx_h = (sem(f"ctx_{s}") for s in ("mv", "rstd", "n", "T", "h"))
        ln_mv, ln_rstd, ln_xn, ln_T = (sem(f"ln_{s}") for s in ("mv", "rstd", "xn", "T"))
        ln_hA, ln_hD = sem("ln_hA"), sem("ln_hD")
        scores, rowmax, exps, recips, norms, probs_T, probs_Tc, pv, o_copied = (
            sem(s) for s in ("scores", "rowmax", "exps", "recips", "norms", "probs_T", "probs_Tc", "pv", "o_copied"))
        wo_done = sem("wo_done")
        filled, fill_out = [[sem(f"{s}_{f}") for f in FILLS] for s in ("filled", "fill_out")]
        swapped, rope_cos, rope_sin, roped = (
            [sem(f"{s}_{f}") for f in FILLS[:4]] for s in ("swapped", "rope_cos", "rope_sin", "roped"))
        acc_done = sem("acc_done")
        x_sum = sem("x_sum")
        x_done = sem("x_done")
        a_scores, a_rowmax, a_exps, a_T, a_pv, a_ev, a_back, a_rzo, a_norm, a_km, a_vst = (
            sem(f"a_{s}") for s in ("scores", "rowmax", "exps", "T", "pv", "ev", "back", "rzo", "norm", "km", "vst"))
        a_Tc = [sem("a_Tc_even"), sem("a_Tc_odd")]
        pre, pre_out = sem("pre"), sem("pre_out")
        end_ev, end_back, end_rzo, end_norm = (sem(f"end_{s}") for s in ("ev", "back", "rzo", "norm"))
        post_T, post_oT = sem("post_T"), sem("post_oT")
        ffn_h, ffn_g = sem("ffn_h"), sem("ffn_g")
        stored = sem("stored")

        PRE0 = [("ctx1", 0, 5), ("ctx1", 1, 5), ("ck", 0, 5), ("ck", 1, 5), ("cv", 0, 5), ("cv", 1, 5)]
        PRE1 = [("k", 0, 4), ("q", 0, 5), ("v", 0, 2), ("k", 1, 3), ("q", 1, 4), ("v", 1, 5)]
        PRE2 = [("cq", 0, 4), ("cq", 1, 5)]
        PRE = PRE0 + PRE1 + PRE2
        NPRE = [len(PRE0), len(PRE0) + len(PRE1), len(PRE)]
        MLP_BANKS = [4, 5, 2, 3]
        POOL_SUMS = (2, 3)
        END_O, END_BACK = (6, 0), (7, 1)
        FIRST_BANKS = [5, 4, 0, 1, 2, 3]
        LN_BANKS = [(2, 3), (0, 1)]
        MODS = [0, 0, 2, 4, 6, 8]

        def slots(n, is_last, a):
            if not is_last:
                return [("fill", n + 1, f) for f in range(6)]
            if a == 0:
                return [("fill", STEPS, f) for f in (1, 3, 4, 5)]
            return [("pre", j, None) for j in range(len(PRE0))]

        def head_pairs(eng, first, step):
            step(first, first % 2, True, False)
            with eng.Fori(0, (STEPS - 2) // 2) as r:
                for p in range(2):
                    step(r * 2 + (first + 1 + p), (first + 1 + p) % 2, False, False)
            step(first + STEPS - 1, (first + STEPS - 1) % 2, False, True)

        block = es.enter_context(nc.Block())

        @block.sync
        def _(sp):
            for half in range(2):
                b0 = HALF * half
                sp.dma_start(x[:, b0:b0 + HALF, :], x_in[b0:b0 + HALF, :, :].rearrange("b t d -> t b d")).then_inc(
                    ld_x[half], 16)
            sp.dma_start(wqkv[:, 0, :], wqkv_in[0, :, :]).then_inc(ld_wqkv[0], 16)
            sp.dma_start(wqkv[:, 1, :], wqkv_in[1, :, :]).then_inc(ld_wqkv[1], 16)
            sp.dma_start(wo[:, 0, :], wo_in[0, :, :]).then_inc(ld_wo[0], 16)
            sp.dma_start(wo[:, 1, :], wo_in[1, :, :]).then_inc(ld_wo[1], 16)
            sp.dma_start(ctx[:, :, :], ctx_in.rearrange("b t d -> t b d")).then_inc(ld_ctx, 16)
            sp.dma_start(ctxT[:, :], ctxT_in).then_inc(ld_ctxT, 16)
            sp.dma_start(wsq[:, :], wsq_in).then_inc(ld_sq, 16)
            sp.dma_start(wff[:, :], wff_in).then_inc(ld_ff, 16)
            sp.wait_ge(row_part, 5)
            for j in range(3):
                sp.dma_start(parts_row[j:j + 1, :], parts[:, j, :]).then_inc(row_moved, 16)

            def swap(m, f):
                sp.wait_ge(fill_out[f], m + 1)
                for e in range(2):
                    sp.dma_start(swp[e:P:2, f, :], raw[1 - e:P:2, f, :]).then_inc(swapped[f], 16)

            def load_wqkv(n, p):
                for f in range(6):
                    sp.wait_ge(filled[f], n + 1)
                sp.dma_start(wqkv[:, p, :], wqkv_in[bass.ds(n + 2, 1), :, :].rearrange("o p c -> p (o c)")).then_inc(
                    ld_wqkv[p], 16)

            def load_wo(n, p):
                sp.wait_ge(wo_done, n * 2)
                sp.dma_start(wo[:, 1 - p, :], wo_in[bass.ds(n + 1, 1), :, :].rearrange("o p c -> p (o c)")).then_inc(
                    ld_wo[1 - p], 16)

            def l0_step(n, p, is_first, is_last, a):
                if not (a == 1 and is_last):
                    load_wqkv(n, p)
                for kind, m, f in slots(n, is_last, a):
                    if kind == "fill" and f < 4:
                        swap(m, f)
                if not (a == 0 and is_first) and not (a == 1 and is_last):
                    load_wo(n, p)

            for a in range(2):
                for f in range(0, 4, 1 + a):
                    swap(STEPS * a, f)
                head_pairs(sp, STEPS * a, partial(l0_step, a=a))
            for half in range(2):
                b0 = HALF * half
                sp.wait_ge(x_done, half + 1)
                sp.dma_start(out[b0:b0 + HALF, :, :].rearrange("b t d -> t b d"), x[:, b0:b0 + HALF, :]).then_inc(
                    stored, 16)
            sp.wait_ge(stored, 32)

        @block.gpsimd
        def _(pool):
            pool.dma_start(rows[:, :], row_in).then_inc(ld_rows, 16)
            for p in range(2):
                pool.memset(vst[:, p, :, :, DH1 + 1:VW], 0.0).then_inc(presets, 1)
                pool.memset(vst[:, p, :, :, DH1:DH1 + 1], 1.0).then_inc(presets, 1)

            def inv_std(k):
                for half in range(2):
                    cols = slice(HALF * half, HALF * (half + 1))
                    pool.wait_ge(ln_mv, 2 * k + half + 1)
                    nc.gpsimd.tensor_tensor(rstd[:, 0, cols], vare[:, 0, cols], neg_half[:, cols], ALU.pow).then_inc(
                        ln_rstd, 1)

            def rope_sum(m, f, mp):
                pool.wait_ge(rope_sin[f], m + 1)
                pool.wait_ge(rope_cos[f], m + 1)
                nc.gpsimd.tensor_tensor(qk[:, mp, f, :], qk[:, mp, f, :], swp[:, f, :], ALU.add).then_inc(roped[f], 1)

            def rope_sine(m, f):
                pool.wait_ge(swapped[f], m * 32 + 32)
                nc.gpsimd.tensor_tensor(four(swp[:, f, :]), four(swp[:, f, :]), sin, ALU.mult).then_inc(rope_sin[f], 1)

            def l0_step(n, p, is_first, is_last, a):
                for kind, m, f in slots(n, is_last, a):
                    if kind == "fill" and f < 4:
                        rope_sine(m, f)
                        if f in POOL_SUMS:
                            rope_sum(m, f, 1 - p)

            def split_rows():
                pool.wait_ge(ld_rows, 16)
                src, done = rows, 0
                for j in range(3):
                    nc.gpsimd.tensor_copy(parts[:, j, :], src[:, :]).then_inc(row_part, 1)
                    done += 1
                    pool.wait_ge(row_part, done)
                    if j < 2:
                        nc.gpsimd.tensor_tensor(rest[:, :], src[:, :], parts[:, j, :], ALU.subtract).then_inc(row_part, 1)
                        done += 1
                        pool.wait_ge(row_part, done)
                        src = rest

            def stage_values(m, p, a):
                pool.wait_ge(presets, 5)
                if not (isinstance(m, int) and m < 2):
                    pool.wait_ge(a_pv, m * 4 - 4)
                src = v1[:, a, :, bass.ds(m * (2 * DH1) - a * P, 2 * DH1)].rearrange("p b (h d) -> p b h d", h=2)
                nc.gpsimd.tensor_copy(vst[:, p, :, :, 0:DH1], src).then_inc(a_vst, 1)

            def l1_step(n, p, is_first, is_last, a):
                if not is_last:
                    stage_values(n + 1, 1 - p, a)

            inv_std(0)
            split_rows()
            pool.wait_ge(ctx_mv, 1)
            nc.gpsimd.tensor_tensor(rstd[:, 1, :], vare[:, 1, :], neg_half[:, :], ALU.pow).then_inc(ctx_rstd, 1)
            for a in range(2):
                if a:
                    inv_std(1)
                for f in range(0, 4, 1 + a):
                    rope_sine(STEPS * a, f)
                head_pairs(pool, STEPS * a, partial(l0_step, a=a))
            inv_std(2)
            for a in range(2):
                if a == 0:
                    inv_std(3)
                    pool.wait_ge(pre_out, NPRE[1])
                stage_values(STEPS * a, 0, a)
                if a:
                    inv_std(4)
                head_pairs(pool, STEPS * a, partial(l1_step, a=a))
            inv_std(5)

        @block.scalar
        def _(act):
            act.dma_start(small[:, :], small_in).then_inc(ld_small, 16)
            act.dma_start(wmod[:, :], wmod_in).then_inc(ld_mod, 16)
            act.wait_ge(ld_small, 16)
            nc.scalar.activation(silu[:, 0, :], condT, ACT.Exp, scale=-1.0).then_inc(exp_c, 1)

            def load_table(func):
                nc.scalar.activation(primer[:, :], small[:, 0:1], func)

            def ln_scale_shift(k):
                for half in range(2):
                    act.wait_ge(ln_T, 4 * k + 2 * half + 1)
                    ps, b0 = bank[LN_BANKS[half][0]], HALF * half
                    if k == 0 and half == 0:
                        act.wait_ge(mod_done, 1)
                    j = MODS[k]
                    for u in range(2):
                        b = b0 + u
                        last = nc.scalar.activation(hT[:, b * P:(b + 1) * P], ps[:, u * P:(u + 1) * P],
                                                    ACT.Identity, bias=mod[:, j + 1, b:b + 1], scale=mod[:, j, b:b + 1])
                    last.then_inc(ln_hA, 1)

            def evacuate_fill(m, f, mp, src=5):
                act.wait_ge(filled[f], m + 1)
                if f < 4:
                    if not (isinstance(m, int) and m == 0):
                        act.wait_ge(roped[f], m)
                    ins = nc.scalar.activation(raw[:, f, :], bank[src][:, :], ACT.Copy,
                                               scale=DH0 ** -0.5 if f in (0, 2) else 1.0)
                else:
                    ins = nc.scalar.activation(v0[:, mp, (f - 4) * BANK:(f - 3) * BANK], bank[src][:, :], ACT.Copy)
                ins.then_inc(fill_out[f], 1)

            def exp0(n, g):
                act.wait_ge(rowmax, n * 4 + (g + 1))
                for u in range(HALF):
                    c = g * HALF + u
                    last = nc.scalar.activation(prob[:, g, u * P:(u + 1) * P], bank[g % 2][:, u * P:(u + 1) * P],
                                                ACT.Exp, bias=nmax[:, c:c + 1], accum_out=zsum[:, c:c + 1])
                last.then_inc(exps, 1)

            def evacuate_o(n, half):
                act.wait_ge(pv, n * 2 + (half + 1))
                nc.scalar.activation(oT[:, half * BANK:(half + 1) * BANK], bank[4][:, :], ACT.Copy).then_inc(o_copied, 1)

            def l0_step(n, p, is_first, is_last, a):
                todo = slots(n, is_last, a)

                def slot(k):
                    if k < len(todo):
                        kind, m, f = todo[k]
                        evacuate_fill(m, f, 1 - p) if kind == "fill" else pre_evacuate(m)

                slot(0)
                exp0(n, 0)
                slot(1)
                slot(2)
                exp0(n, 1)
                if not is_first:
                    evacuate_o(n - 1, 1)
                slot(3)
                exp0(n, 2)
                exp0(n, 3)
                slot(4)
                if not is_last:
                    slot(5)
                evacuate_o(n, 0)
                if is_last:
                    slot(5)
                    evacuate_o(n, 1)

            def pre_evacuate(j):
                what, half, ps = PRE[j]
                act.wait_ge(pre, j + 1)
                src = bank[ps][:, :]
                cols = slice(half * BANK, (half + 1) * BANK)
                if what == "ctx1":
                    ins = nc.scalar.activation(ctx1T[:, cols], src, ACT.Identity, bias=vcol("b_ctx"))
                elif what == "q":
                    ins = nc.scalar.activation(q1[:, cols], src, ACT.Identity, bias=bq_scaled[:, :], scale=DH1 ** -0.5)
                elif what == "cq":
                    ins = nc.scalar.activation(q1[:, cols], src, ACT.Copy, scale=DH1 ** -0.5)
                elif what == "k":
                    ins = nc.scalar.activation(k1[:, 0, cols], src, ACT.Identity, bias=vcol("b_k"))
                elif what == "ck":
                    ins = nc.scalar.activation(k1[:, 1, cols], src, ACT.Copy)
                else:
                    a = 0 if what == "v" else 1
                    ins = nc.scalar.activation(v1[:, a, HALF * half:HALF * (half + 1), :], four(src), ACT.Copy)
                ins.then_inc(pre_out, 1)

            def gelu(k, func, bias):
                base = 0 if k == 2 else 2 * FF
                for j in range(2 * FF):
                    c, half = j % FF, j // FF
                    act.wait_ge(ffn_h, base + j + 1)
                    nc.scalar.activation(gT[:, c, half * BANK:(half + 1) * BANK], bank[MLP_BANKS[j % 4]][:, :], func,
                                         bias=vcol(f"{bias}{c}")).then_inc(ffn_g, 1)

            def exp1(n, g):
                act.wait_ge(a_rowmax, n * 4 + (g + 1))
                for u in range(HALF):
                    c = g * HALF + u
                    last = nc.scalar.activation(prob[:, g, u * P:(u + 1) * P], bank[g][:, u * P:(u + 1) * P],
                                                ACT.Exp, bias=nmax[:, c:c + 1])
                last.then_inc(a_exps, 1)

            def copy_T(n, g):
                act.wait_ge(a_T, n * 4 + (g + 1))
                nc.scalar.activation(probT[:, g, :], bank[4 + g % 2][:, :], ACT.Copy).then_inc(a_Tc[1], 1)

            def evacuate_o1(n):
                act.wait_ge(a_pv, n * 4 + 4)
                nc.scalar.activation(oS[:, :], bank[6][:, :], ACT.Copy).then_inc(a_ev, 1)

            def evacuate_o1_half(n, a, half):
                if half == 0:
                    act.wait_ge(a_back, n)
                act.wait_ge(a_pv, n * 4 + (2 * half + 2))
                nc.scalar.activation(by_half(oS)[:, :, half, :], by_half(bank[END_O[half]])[:, :, half, :],
                                     ACT.Copy).then_inc(a_ev if half else end_ev, 1)

            def l1_step(n, p, is_first, is_last, a):
                if is_first:
                    exp1(n, 0)
                else:
                    copy_T(n - 1, 3)
                exp1(n, 1)
                if not is_first:
                    evacuate_o1(n - 1)
                exp1(n, 2)
                copy_T(n, 1)
                exp1(n, 3)
                if not is_last:
                    exp1(n + 1, 0)
                else:
                    evacuate_o1_half(n, a, 0)
                    copy_T(n, 3)
                    evacuate_o1_half(n, a, 1)

            def evacuate_post(a):
                for half in range(2):
                    act.wait_ge(post_T, 2 * a + half + 1)
                    dst, src = oT[:, half * BANK:(half + 1) * BANK], bank[4 + half][:, :]
                    if a == 0:
                        ins = nc.scalar.activation(dst, src, ACT.Identity, bias=vcol("b_v"))
                    else:
                        ins = nc.scalar.activation(dst, src, ACT.Copy)
                    ins.then_inc(post_oT, 1)

            for a in range(2):
                ln_scale_shift(a)
                for f in (range(6) if a == 0 else (0, 2)):
                    evacuate_fill(STEPS * a, f, 0, FIRST_BANKS[f])
                if a == 0:
                    act.wait_ge(ctx_T, 1)
                    nc.scalar.activation(ctxnT[:, 0:BANK], bank[6][0:DC, :], ACT.Identity, bias=vcol("lnc_b", DC),
                                         scale=vcol("lnc_w", DC)).then_inc(ctx_h, 1)
                head_pairs(act, STEPS * a, partial(l0_step, a=a))
            load_table(ACT.Gelu)
            ln_scale_shift(2)
            gelu(2, ACT.Gelu, "ffb")
            load_table(ACT.Exp)
            for a in range(2):
                ln_scale_shift(3 + a)
                for j in range(NPRE[a], NPRE[a + 1]):
                    pre_evacuate(j)
                head_pairs(act, STEPS * a, partial(l1_step, a=a))
                evacuate_post(a)
            load_table(ACT.Gelu_apprx_tanh)
            ln_scale_shift(5)
            gelu(5, ACT.Gelu_apprx_tanh, "fcb")

        @block.vector
        def _(dve):
            links = [0]

            def link(ins):
                links[0] += 1
                ins.then_inc(dve_link, 1)
                dve.wait_ge(dve_link, links[0])

            nc.vector.memset(ones[:, :], 1.0).then_inc(presets, 1)
            nc.vector.memset(neg_half[:, :], -0.5)

            def statistics(c, src, b0, b1, eps):
                for b in range(b0, b1):
                    last = nc.vector.bn_stats(st[:, c, b, :], src[:, b, :])
                link(last)
                for b in range(b0, b1):
                    last = nc.vector.bn_aggr(mv[:, c, b, :], st[:, c, b, :])
                link(last)
                return nc.vector.tensor_scalar(vare[:, c, b0:b1], mv[:, c, b0:b1, 1], eps, None, ALU.add)

            def ln_stats(k, half):
                statistics(0, x, HALF * half, HALF * (half + 1), EPS0 if k < 3 else EPS1).then_inc(ln_mv, 1)

            def ln_normalise(k, half):
                if k and half == 0:
                    dve.wait_ge(ln_T, 4 * k)
                dve.wait_ge(ln_rstd, 2 * k + half + 1)
                for b in range(HALF * half, HALF * (half + 1)):
                    last = nc.vector.tensor_scalar(xn[:, b, :], x[:, b, :], mv[:, 0, b, 0:1], rstd[:, 0, b:b + 1],
                                                   ALU.subtract, ALU.mult)
                last.then_inc(ln_xn, 1)

            def ln_scale_shift(k, half):
                dve.wait_ge(ln_T, 4 * k + 2 * half + 2)
                ps, b0, j = bank[LN_BANKS[half][1]], HALF * half + 2, MODS[k]
                for u in range(2):
                    b = b0 + u
                    last = nc.vector.tensor_scalar(hT[:, b * P:(b + 1) * P], ps[:, u * P:(u + 1) * P],
                                                   mod[:, j, b:b + 1], mod[:, j + 1, b:b + 1], ALU.mult, ALU.add)
                last.then_inc(ln_hD, 1)

            def context_norm():
                dve.wait_ge(ctx_rstd, 1)
                for b in range(B):
                    last = nc.vector.tensor_scalar(ctx[:, b, :], ctx[:, b, :], mv[:, 1, b, 0:1], rstd[:, 1, b:b + 1],
                                                   ALU.subtract, ALU.mult)
                last.then_inc(ctx_n, 1)

            def residual(half, sublayer):
                xs = x[:, HALF * half:HALF * (half + 1), :]
                if sublayer < 2:
                    dve.wait_ge(wo_done, 2 * STEPS * (sublayer + 1) - 1 + half)
                else:
                    dve.wait_ge(acc_done, 2 * (sublayer - 2) + half + 1)
                ins = nc.vector.tensor_tensor(xs, xs, four(bank[6 + half][:, :]), ALU.add)
                if sublayer == 5:
                    ins.then_inc(x_done, 1)
                else:
                    ins.then_inc(x_sum, 1)
                    dve.wait_ge(x_sum, 2 * sublayer + half + 1)

            def layer_norm(k, begun):
                if not begun:
                    residual(0, k - 1)
                    ln_stats(k, 0)
                ln_normalise(k, 0)
                residual(1, k - 1)
                ln_scale_shift(k, 0)
                ln_stats(k, 1)
                ln_normalise(k, 1)
                ln_scale_shift(k, 1)

            def silu_condition():
                dve.wait_ge(exp_c, 1)
                link(nc.vector.tensor_scalar(silu[:, 1, :], silu[:, 0, :], 1.0, None, ALU.add))
                link(nc.vector.reciprocal(silu[:, 2, :], silu[:, 1, :]))
                nc.vector.tensor_tensor(silu[:, 3, :], silu[:, 2, :], condT, ALU.mult).then_inc(silu_done, 1)

            def modulation():
                nc.vector.tensor_scalar(bq_scaled[:, :], vcol("b_q"), DH1 ** -0.5, None, ALU.mult)
                dve.wait_ge(mod_ps, 1)
                bias = small[:, VEC:VEC + NMOD].unsqueeze(2).broadcast_to([P, NMOD, B])
                link(nc.vector.tensor_tensor(mod[:, :, :], bank[6][:, 0:NMOD * B].rearrange("p (j b) -> p j b", j=NMOD),
                                             bias, ALU.add))
                link(nc.vector.tensor_scalar(mod[:, 0:NMOD:2, :], mod[:, 0:NMOD:2, :], 1.0, None, ALU.add))
                for j, ln in ((0, "ln1"), (2, "ln2")):
                    last = nc.vector.scalar_tensor_tensor(mod[:, j + 1, :], mod[:, j, :], vcol(f"{ln}_b"), mod[:, j + 1, :],
                                                          ALU.mult, ALU.add)
                link(last)
                for j, ln in ((0, "ln1"), (2, "ln2")):
                    last = nc.vector.tensor_scalar(mod[:, j, :], mod[:, j, :], vcol(f"{ln}_w"), None, ALU.mult)
                link(last)
                nc.vector.engine_nop().then_inc(mod_done, 1)

            def row_max(n, g):
                dve.wait_ge(scores, n * 4 + (g + 1))
                nc.vector.tensor_reduce(nmax[:, g * HALF:(g + 1) * HALF], four(bank[g % 2][:, :]), AX.X, ALU.max,
                                        negate=True).then_inc(rowmax, 1)

            def normalise(n, g):
                dve.wait_ge(exps, n * 4 + (g + 1))
                cols = slice(g * HALF, (g + 1) * HALF)
                nc.vector.reciprocal(rz[:, cols], zsum[:, cols]).then_inc(recips, 1)
                dve.wait_ge(recips, n * 4 + (g + 1))
                nc.vector.tensor_tensor(four(prob[:, g, :]), four(prob[:, g, :]),
                                        rz[:, cols].unsqueeze(2).broadcast_to([P, HALF, P]), ALU.mult).then_inc(norms, 1)

            def copy_T0(n, g):
                dve.wait_ge(probs_T, n * 4 + (g + 1))
                nc.vector.tensor_copy(probT[:, g, :], bank[2 + g % 2][:, :]).then_inc(probs_Tc, 1)

            def rope_cosine(m, f, mp):
                dve.wait_ge(fill_out[f], m + 1)
                nc.vector.tensor_tensor(four(qk[:, mp, f, :]), four(raw[:, f, :]), cos, ALU.mult).then_inc(rope_cos[f], 1)

            def rope_sum(m, f, mp):
                dve.wait_ge(rope_sin[f], m + 1)
                dve.wait_ge(rope_cos[f], m + 1)
                nc.vector.tensor_tensor(qk[:, mp, f, :], qk[:, mp, f, :], swp[:, f, :], ALU.add).then_inc(roped[f], 1)

            def l0_step(n, p, is_first, is_last, a):
                todo = [(m, f) for kind, m, f in slots(n, is_last, a) if kind == "fill" and f < 4]

                def cosine(k):
                    if k < len(todo):
                        rope_cosine(*todo[k], 1 - p)

                def total(k):
                    if k < len(todo) and todo[k][1] not in POOL_SUMS:
                        rope_sum(*todo[k], 1 - p)

                row_max(n, 0)
                row_max(n, 1)
                cosine(0)
                normalise(n, 0)
                copy_T0(n, 0)
                row_max(n, 2)
                cosine(1)
                normalise(n, 1)
                row_max(n, 3)
                normalise(n, 2)
                copy_T0(n, 1)
                normalise(n, 3)
                cosine(2)
                total(0)
                total(1)
                cosine(3)
                copy_T0(n, 2)
                copy_T0(n, 3)
                if is_last:
                    residual(0, a)
                    ln_stats(a + 1, 0)

            def mask_keys(m, p, a, hh):
                nc.vector.tensor_scalar(km[:, p, hh, :], k1[:, a, :], small[:, bass.ds(m * 2 + (MASK + hh - a * H), 1)],
                                        None, ALU.mult).then_inc(a_km, 1)

            def row_max1(n, g):
                dve.wait_ge(a_scores, n * 4 + (g + 1))
                nc.vector.tensor_reduce(nmax[:, g * HALF:(g + 1) * HALF], four(bank[g][:, :]), AX.X, ALU.max,
                                        negate=True).then_inc(a_rowmax, 1)

            def copy_T1(n, g):
                dve.wait_ge(a_T, n * 4 + (g + 1))
                nc.vector.tensor_copy(probT[:, g, :], bank[4 + g % 2][:, :]).then_inc(a_Tc[0], 1)

            def divide(n, a):
                dve.wait_ge(a_back, n + 1)
                src = bank[7][:, :].rearrange("p (h b v) -> p h b v", h=2, b=B)
                nc.vector.reciprocal(rzo[:, :].rearrange("p (h b) -> p h b", h=2), src[:, :, :, DH1]).then_inc(a_rzo, 1)
                dve.wait_ge(a_rzo, n + 1)
                dst = oN[:, :, bass.ds(n * (2 * DH1) - a * P, 2 * DH1)].rearrange("p b (h d) -> p h b d", h=2)
                nc.vector.tensor_tensor(dst, src[:, :, :, 0:DH1], rzo[:, :].rearrange("p (h b) -> p h b", h=2).unsqueeze(3)
                                        .broadcast_to([P, 2, B, DH1]), ALU.mult).then_inc(a_norm, 1)

            def divide_half(n, a, half):
                back, recip, norm, count = (a_back, a_rzo, a_norm, n + 1) if half else (end_back, end_rzo, end_norm, a + 1)
                hb = slice(HALF * half, HALF * (half + 1))
                dve.wait_ge(back, count)
                src = bank[END_BACK[half]][:, :].rearrange("p (h b v) -> p h b v", h=2, b=B)[:, :, hb, :]
                rz_half = rzo[:, :].rearrange("p (h b) -> p h b", h=2)[:, :, hb]
                nc.vector.reciprocal(rz_half, src[:, :, :, DH1]).then_inc(recip, 1)
                dve.wait_ge(recip, count)
                dst = oN[:, hb, (n - STEPS * a) * 2 * DH1:(n - STEPS * a + 1) * 2 * DH1].rearrange(
                    "p b (h d) -> p h b d", h=2)
                nc.vector.tensor_tensor(dst, src[:, :, :, 0:DH1], rz_half.unsqueeze(3).broadcast_to([P, 2, HALF, DH1]),
                                        ALU.mult).then_inc(norm, 1)

            def l1_step(n, p, is_first, is_last, a):
                if is_first:
                    for g in range(3):
                        row_max1(n, g)
                if not is_last:
                    mask_keys(n + 1, 1 - p, a, 0)
                row_max1(n, 3)
                if not is_last:
                    mask_keys(n + 1, 1 - p, a, 1)
                copy_T1(n, 0)
                if not is_last:
                    row_max1(n + 1, 0)
                    row_max1(n + 1, 1)
                copy_T1(n, 2)
                if not is_first:
                    divide(n - 1, a)
                if not is_last:
                    row_max1(n + 1, 2)
                else:
                    for half in range(2):
                        divide_half(n, a, half)

            dve.wait_ge(ld_small, 16)
            silu_condition()
            for half in range(2):
                dve.wait_ge(ld_x[half], 16)
                ln_stats(0, half)
            ln_normalise(0, 0)
            modulation()
            ln_normalise(0, 1)
            for half in range(2):
                ln_scale_shift(0, half)
            dve.wait_ge(ld_ctx, 16)
            statistics(1, ctx, 0, B, EPS0).then_inc(ctx_mv, 1)
            for a in range(2):
                if a:
                    layer_norm(1, True)
                for f in range(0, 4, 1 + a):
                    rope_cosine(STEPS * a, f, 0)
                if a == 0:
                    context_norm()
                for f in range(0, 4, 1 + a):
                    rope_sum(STEPS * a, f, 0)
                if a == 0:
                    dve.wait_ge(ctx_T, 2)
                    nc.vector.tensor_scalar(ctxnT[:, BANK:2 * BANK], bank[7][0:DC, :], vcol("lnc_w", DC),
                                            vcol("lnc_b", DC), ALU.mult, ALU.add).then_inc(ctx_h, 1)
                head_pairs(dve, STEPS * a, partial(l0_step, a=a))
            layer_norm(2, True)
            for a in range(2):
                if a == 0:
                    layer_norm(3, False)
                    dve.wait_ge(pre_out, NPRE[0] + 4)
                for hh in range(2):
                    mask_keys(STEPS * a, 0, a, hh)
                if a:
                    layer_norm(4, False)
                head_pairs(dve, STEPS * a, partial(l1_step, a=a))
            layer_norm(5, False)
            for half in range(2):
                residual(half, 5)

        @block.tensor
        def _(pe):
            def mm(o, lhsT, rhs, start, stop):
                return nc.tensor.matmul(o, lhsT, rhs, start=start, stop=stop, skip_group_check=True)

            def bcols(b):
                return slice(b * P, (b + 1) * P)

            def transpose_norm(k, half):
                pe.wait_ge(ln_xn, 2 * k + half + 1)
                if k:
                    pe.wait_ge(ln_hA, 2 * k + half - 1)
                    pe.wait_ge(ln_hD, 2 * k + half - 1)
                for e in range(2):
                    for u in range(2):
                        last = nc.tensor.transpose(bank[LN_BANKS[half][e]][:, bcols(u)],
                                                   xn[:, HALF * half + 2 * e + u, :], ident)
                    last.then_inc(ln_T, 1)

            def wait_hT(k, half):
                pe.wait_ge(ln_hA, 2 * k + half + 1)
                pe.wait_ge(ln_hD, 2 * k + half + 1)

            def seed(name, half):
                pe.wait_ge(row_moved, 48)
                cols = slice(ROWS[name] * P, (ROWS[name] + 1) * P)
                mm(four(bank[6 + half][:, :]), ones[:, :],
                   parts_row[:, cols].unsqueeze(1).broadcast_to([3, HALF, P]), start=True, stop=False)

            def fill(m, f, mp, a, k=None, ps=5, after=None):
                kv, width = (hT, P) if a == 0 else (ctxnT, DC)
                half = f - 4 if f > 3 else f // 2
                if k is not None:
                    wait_hT(k, half)
                pe.wait_ge(ld_wqkv[mp], m * 8 + (16 - 8 * mp))
                if after is not None:
                    pe.wait_ge(fill_out[after[1]], after[0] + 1)
                cols = slice(half * BANK, (half + 1) * BANK)
                if f in (0, 2):
                    last = mm(bank[ps][:, :], wqkv[:, mp, 0:P], hT[:, cols], True, True)
                elif f in (1, 3):
                    last = mm(bank[ps][:, :], wqkv[0:width, mp, P:2 * P], kv[:, cols], True, True)
                else:
                    for u in range(HALF):
                        last = mm(bank[ps][:, bcols(u)], kv[:, bcols(HALF * half + u)], wqkv[0:width, mp, 2 * P:3 * P],
                                  True, True)
                last.then_inc(filled[f], 1)

            def score(n, p, g, lead):
                hh, half = g % 2, g // 2
                pe.wait_ge(roped[2 * half], n + 1)
                pe.wait_ge(roped[2 * half + 1], n + 1)
                if lead:
                    pe.wait_ge(fill_out[2 + g], n + 1)
                else:
                    pe.wait_ge(exps, n * 4 + (g - 1))
                lanes = slice(DH0 * hh, DH0 * (hh + 1))
                for u in range(HALF):
                    last = mm(bank[g % 2][:, bcols(u)], qk[lanes, p, 2 * half, bcols(u)],
                              qk[lanes, p, 2 * half + 1, bcols(u)], True, True)
                last.then_inc(scores, 1)

            def transpose_probs(n, g, is_first):
                pe.wait_ge(norms, n * 4 + (g + 1))
                if g >= 2 or not is_first:
                    pe.wait_ge(probs_Tc, n * 4 + (g - 1))
                else:
                    pe.wait_ge(fill_out[4 + g], n + 1)
                for u in range(HALF):
                    last = nc.tensor.transpose(bank[2 + g % 2][:, bcols(u)], prob[:, g, bcols(u)], ident)
                last.then_inc(probs_T, 1)

            def prob_values(n, p, half, is_first):
                pe.wait_ge(probs_Tc, n * 4 + (2 * half + 2))
                pe.wait_ge(fill_out[4 + half], n + 1)
                if half or not is_first:
                    pe.wait_ge(o_copied, n * 2 + half)
                for u in range(HALF):
                    for hh in range(2):
                        b = HALF * half + u
                        last = mm(bank[4][DH0 * hh:DH0 * (hh + 1), bcols(u)],
                                  v0[:, p, b * P + DH0 * hh:b * P + DH0 * (hh + 1)], probT[:, 2 * half + hh, bcols(u)],
                                  True, True)
                last.then_inc(pv, 1)

            def project_out(n, p, half):
                pe.wait_ge(o_copied, n * 2 + (half + 1))
                if half == 0:
                    pe.wait_ge(ld_wo[p], n * 8 + (16 - 8 * p))
                for u in range(HALF):
                    last = mm(bank[6 + half][:, bcols(u)], oT[:, bcols(HALF * half + u)], wo[:, p, :], False, False)
                last.then_inc(wo_done, 1)

            def l0_step(n, p, is_first, is_last, a):
                todo = slots(n, is_last, a)

                def slot(k):
                    if k >= len(todo):
                        return
                    kind, m, f = todo[k]
                    if kind == "fill":
                        fill(m, f, 1 - p, a if not is_last else 1, after=(n, 5) if k == 0 else (m, todo[k - 1][2]))
                    else:
                        pre_fill(m)

                score(n, p, 0, is_first)
                slot(0)
                score(n, p, 1, is_first)
                slot(1)
                if not is_first:
                    prob_values(n - 1, 1 - p, 1, False)
                slot(2)
                transpose_probs(n, 0, is_first)
                score(n, p, 2, False)
                slot(3)
                score(n, p, 3, False)
                if not is_first:
                    project_out(n - 1, 1 - p, 0)
                transpose_probs(n, 1, is_first)
                slot(4)
                if not is_first:
                    project_out(n - 1, 1 - p, 1)
                prob_values(n, p, 0, is_first)
                slot(5)
                transpose_probs(n, 2, is_first)
                if is_last:
                    project_out(n, p, 0)
                transpose_probs(n, 3, is_first)
                if is_first:
                    if a:
                        pe.wait_ge(x_sum, 2)
                    else:
                        pe.wait_ge(ctx_h, 2)
                    for half in range(2):
                        seed("sa_bo" if a == 0 else "ca_bo", half)
                if is_last:
                    prob_values(n, p, 1, False)
                    project_out(n, p, 1)

            def pre_fill(j):
                what, half, ps = PRE[j]
                same = [i for i in range(j) if PRE[i][2] == ps]
                if same:
                    pe.wait_ge(pre_out, same[-1] + 1)
                if j == 0:
                    pe.wait_ge(ld_sq, 16)
                    pe.wait_ge(ld_ctxT, 16)
                    pe.wait_ge(fill_out[5], 2 * STEPS)
                if what in ("ck", "cv"):
                    pe.wait_ge(pre_out, half + 1)
                if what in ("q", "k", "v"):
                    wait_hT(3, half)
                if what == "cq":
                    wait_hT(4, half)
                w = wsq[0:DC if what == "ctx1" else P, SQ["ctx" if what == "ctx1" else what] * P:][:, 0:P]
                src = {"ctx1": ctxT, "ck": ctx1T, "cv": ctx1T}.get(what, hT)
                if what in ("v", "cv"):
                    for u in range(HALF):
                        last = mm(bank[ps][:, bcols(u)], src[:, bcols(HALF * half + u)], w, True, True)
                else:
                    last = mm(bank[ps][:, :], w, src[:, half * BANK:(half + 1) * BANK], True, True)
                last.then_inc(pre, 1)

            def score1(n, p, g, lead):
                hh, half = g % 2, g // 2
                pe.wait_ge(a_km, n * 2 + (hh + 1))
                if not lead:
                    pe.wait_ge(a_exps, n * 4 + (g - 3))
                for u in range(HALF):
                    b = HALF * half + u
                    last = mm(bank[g][:, bcols(u)], q1[:, bcols(b)], km[:, p, hh, bcols(b)], True, True)
                last.then_inc(a_scores, 1)

            def transpose1(n, g, lead):
                pe.wait_ge(a_exps, n * 4 + (g + 1))
                if g >= 2:
                    pe.wait_ge(a_Tc[g % 2], n * 2 + (g // 2))
                elif not lead:
                    pe.wait_ge(a_Tc[g % 2], n * 2)
                for u in range(HALF):
                    last = nc.tensor.transpose(bank[4 + g % 2][:, bcols(u)], prob[:, g, bcols(u)], ident)
                last.then_inc(a_T, 1)

            def prob_values1(n, p, g, lead, ps=6):
                hh, half = g % 2, g // 2
                pe.wait_ge(a_Tc[g % 2], n * 2 + (g // 2 + 1))
                if g == 0:
                    pe.wait_ge(a_vst, n + 1)
                    if not lead:
                        pe.wait_ge(a_ev, n)
                for u in range(HALF):
                    last = mm(bank[ps][VW * u:VW * (u + 1), bcols(2 * hh + half)], vst[:, p, HALF * half + u, hh, :],
                              probT[:, g, bcols(u)], True, True)
                last.then_inc(a_pv, 1)

            def turn_back(n, lead):
                pe.wait_ge(a_ev, n + 1)
                if not lead:
                    pe.wait_ge(a_norm, n)
                for g in range(4):
                    last = nc.tensor.transpose(bank[7][:, bcols(g)], oS[:, bcols(g)], ident)
                last.then_inc(a_back, 1)

            def l1_step(n, p, is_first, is_last, a):
                lead = is_first and a == 0
                if is_first:
                    pe.wait_ge(pre_out, NPRE[a] + (1 if a else 2))
                    for g in range(3):
                        if g == 2:
                            pe.wait_ge(pre_out, NPRE[a + 1])
                        score1(n, p, g, lead)
                score1(n, p, 3, lead)
                transpose1(n, 0, lead)
                if not is_first:
                    prob_values1(n - 1, 1 - p, 3, False)
                if not is_last:
                    score1(n + 1, 1 - p, 0, False)
                transpose1(n, 1, lead)
                prob_values1(n, p, 0, lead)
                if not is_last:
                    score1(n + 1, 1 - p, 1, False)
                transpose1(n, 2, lead)
                prob_values1(n, p, 1, lead)
                if not is_first:
                    turn_back(n - 1, False)
                if not is_last:
                    score1(n + 1, 1 - p, 2, False)
                transpose1(n, 3, lead)
                prob_values1(n, p, 2, lead, END_O[1] if is_last else END_O[0])
                if is_last:
                    turn_back_half(n, a, 0)
                    prob_values1(n, p, 3, lead, END_O[1])
                    attention_T(n, a, 0)
                    seed("b_proj" if a == 0 else "b_out", 0)
                    seed("b_proj" if a == 0 else "b_out", 1)
                    turn_back_half(n, a, 1)
                    project_out1(a, 0)
                    attention_T(n, a, 1)
                    project_out1(a, 1)

            def turn_back_half(n, a, half):
                if half == 0:
                    pe.wait_ge(end_ev, a + 1)
                    pe.wait_ge(a_norm, n)
                else:
                    pe.wait_ge(a_ev, n + 1)
                for hh in range(2):
                    cols = bcols(2 * hh + half)
                    last = nc.tensor.transpose(bank[END_BACK[half]][:, cols], oS[:, cols], ident)
                last.then_inc(a_back if half else end_back, 1)

            def attention_T(n, a, half):
                pe.wait_ge(*((a_norm, n + 1) if half else (end_norm, a + 1)))
                pe.wait_ge(a_Tc[half], (n + 1) * 2)
                for u in range(HALF):
                    last = nc.tensor.transpose(bank[4 + half][:, bcols(u)], oN[:, HALF * half + u, :], ident)
                last.then_inc(post_T, 1)

            def project_out1(a, half):
                w = wsq[:, SQ["proj" if a == 0 else "out"] * P:][:, 0:P]
                pe.wait_ge(post_oT, 2 * a + half + 1)
                for u in range(HALF):
                    last = mm(bank[6 + half][:, bcols(u)], oT[:, bcols(HALF * half + u)], w, False, False)
                last.then_inc(acc_done, 1)

            def mlp(k, name):
                base = 0 if k == 2 else 2 * FF
                off = 0 if k == 2 else 2 * FF * P

                def up(half, c):
                    j = FF * half + c
                    if c == 0:
                        wait_hT(k, half)
                    if j >= 4:
                        pe.wait_ge(ffn_g, base + j - 3)
                    mm(bank[MLP_BANKS[j % 4]][:, :], wff[:, off + c * P:off + (c + 1) * P],
                       hT[:, half * BANK:(half + 1) * BANK], True, True).then_inc(ffn_h, 1)

                def down(half):
                    pe.wait_ge(x_sum, 2 * k - 1 + half)
                    seed(name, half)
                    pe.wait_ge(ffn_g, base + FF * (half + 1))
                    for u in range(HALF):
                        for c in range(FF):
                            last = mm(bank[6 + half][:, bcols(u)], gT[:, c, bcols(HALF * half + u)],
                                      wff[:, off + (FF + c) * P:off + (FF + c + 1) * P], False, False)
                    last.then_inc(acc_done, 1)

                transpose_norm(k, 0)
                for c in range(FF):
                    up(0, c)
                transpose_norm(k, 1)
                up(1, 0)
                down(0)
                for c in range(1, FF):
                    up(1, c)
                down(1)

            pe.wait_ge(ld_small, 16)
            pe.wait_ge(ld_mod, 16)
            pe.wait_ge(silu_done, 1)
            for j in range(NMOD):
                last = mm(bank[6][:, j * B:(j + 1) * B], wmod[:, bcols(j)], condT if j < 4 else silu[:, 3, :], True, True)
            last.then_inc(mod_ps, 1)
            pe.wait_ge(presets, 5)
            for a in range(2):
                for half in range(2):
                    transpose_norm(a, half)
                for f in (range(6) if a == 0 else (0, 2)):
                    fill(STEPS * a, f, 0, a, k=a, ps=FIRST_BANKS[f])
                if a == 0:
                    pe.wait_ge(ctx_n, 1)
                    for half in range(2):
                        for u in range(HALF):
                            last = nc.tensor.transpose(bank[6 + half][0:DC, bcols(u)], ctx[:, HALF * half + u, :], ident)
                        last.then_inc(ctx_T, 1)
                head_pairs(pe, STEPS * a, partial(l0_step, a=a))
            pe.wait_ge(ld_ff, 16)
            mlp(2, "ff_b2")
            for a in range(2):
                for half in range(2):
                    transpose_norm(3 + a, half)
                for j in range(NPRE[a], NPRE[a + 1]):
                    pre_fill(j)
                head_pairs(pe, STEPS * a, partial(l1_step, a=a))
            mlp(5, "b_fc2")


def _packed(i):
    def pad(w):
        return np.concatenate([w, np.zeros((P - w.shape[0], *w.shape[1:]), w.dtype)], axis=0)

    wqkv = []
    for wq, wkv in (("sa_wq", "sa_wkv"), ("ca_wq", "ca_wkv")):
        q, kv = i["L0_xcond_" + wq], pad(i["L0_xcond_" + wkv])
        for s in range(STEPS):
            c = slice(P * s, P * (s + 1))
            wqkv.append(np.concatenate([q[:, c], kv[:, c], kv[:, H * DH0:][:, c]], axis=1))
    wqkv.append(np.zeros_like(wqkv[0]))
    wo = np.concatenate([i["L0_xcond_sa_wo"].reshape(STEPS, P, P), i["L0_xcond_ca_wo"].reshape(STEPS, P, P)], axis=0)
    ada = [i["L1_xcond_W_ada"][:, P * j:P * (j + 1)] for j in (1, 0, 3, 2, 5, 4)]
    wmod = np.concatenate([i["L0_xcond_g1_w"], i["L0_xcond_b1_w"], i["L0_xcond_g2_w"], i["L0_xcond_b2_w"], *ada], axis=1)
    wsq = np.concatenate([i["L1_xcond_W_qkv"], i["L1_xcond_W_proj"], i["L1_xcond_W_q"], i["L1_xcond_W_k"],
                          i["L1_xcond_W_v"], i["L1_xcond_W_out"], pad(i["L1_xcond_W_ctx"])], axis=1)

    def down(w):
        return w.reshape(FF, P, P).transpose(1, 0, 2).reshape(P, FF * P)

    wff = np.concatenate([i["L0_xcond_ff_w1"], down(i["L0_xcond_ff_w2"]), i["L1_xcond_W_fc1"], down(i["L1_xcond_W_fc2"])],
                         axis=1)
    bqkv = i["L1_xcond_b_qkv"].reshape(3, P)
    b_ada = i["L1_xcond_b_ada"].reshape(6, P)
    vecs = [i["L0_xcond_" + n] for n in ("g1_b", "b1_b", "g2_b", "b2_b")] + [b_ada[j] for j in (1, 0, 3, 2, 5, 4)]
    vecs += [i["L0_xcond_" + n] for n in ("ln1_w", "ln1_b", "ln2_w", "ln2_b")]
    vecs += [pad(i["L0_xcond_ca_lnc_w"]), pad(i["L0_xcond_ca_lnc_b"]), bqkv[0], bqkv[1], bqkv[2], i["L1_xcond_b_ctx"]]
    vecs += list(i["L0_xcond_ff_b1"].reshape(FF, P)) + list(i["L1_xcond_b_fc1"].reshape(FF, P))
    rows = np.concatenate([i["L0_xcond_sa_bo"], i["L0_xcond_ca_bo"], i["L0_xcond_ff_b2"], i["L1_xcond_b_proj"],
                           i["L1_xcond_b_out"], i["L1_xcond_b_fc2"]]).reshape(-1, P)
    chan = np.arange(P) % DH0
    inv = (np.float32(1.0) / np.float32(10000.0) ** (np.arange(0, DH0, 2, dtype=np.float32) / np.float32(DH0)))
    ang = (np.arange(P, dtype=np.float32)[:, None] * inv.astype(np.float32)[None, :]).astype(np.float32)
    cos, sin = np.cos(ang).T[chan // 2], np.sin(ang).T[chan // 2]
    sin = np.where(chan[:, None] % 2 == 0, -sin, sin)
    mask = (np.arange(P)[:, None] // DH1 == np.arange(H)[None, :])
    const = np.concatenate([np.eye(P), cos, sin, mask], axis=1).astype(np.float32)
    small = np.concatenate([const, i["cond_1024"].T, np.stack(vecs, axis=1)], axis=1)
    return {
        "small": small, "x": i["x"], "ctx": i["ctx_768"], "ctxT": i["ctx_768"].reshape(B * P, DC).T,
        "wqkv": np.stack(wqkv), "wo": wo, "wmod": wmod, "wsq": wsq, "wff": wff, "row": rows,
    }


def kernel(**inputs):
    import concourse.bacc as bacc
    from concourse.bass_utils import run_bass_kernel_spmd

    nc = bacc.Bacc("TRN2", target_bir_lowering=False, num_devices=1)
    arrays, args = {}, []
    for name, a in _packed({k: np.asarray(v) for k, v in inputs.items()}).items():
        arrays[f"in_{name}"] = np.ascontiguousarray(a)
        args.append(nc.dram_tensor(f"in_{name}", a.shape, F32, kind="ExternalInput").ap())
    args.append(nc.dram_tensor("out_x", (B, P, P), F32, kind="ExternalOutput").ap())
    build(nc, *args)
    return run_bass_kernel_spmd(nc, [arrays], core_ids=[0]).results[0]["out_x"]
```

```python
from contextlib import ExitStack
from functools import partial

import numpy as np

import concourse.bass as bass
from concourse import mybir

F32 = mybir.dt.float32
BF16 = mybir.dt.bfloat16
F32R = mybir.dt.float32r
ALU = mybir.AluOpType
ACT = mybir.ActivationFunctionType
AX = mybir.AxisListType

P = 128
B = 8
HALF = B // 2
BANK = HALF * P
DC = 96
H = 16
DH0 = 64
DH1 = 8
STEPS = H // 2
FF = 4
VW = 32
HW = VW // 2
EPS0, EPS1 = 1e-5, 1e-6

VECS = ["g1_b", "b1_b", "g2_b", "b2_b", "ada1", "ada0", "ada3", "ada2", "ada5", "ada4", "ln1_w", "ln1_b", "ln2_w", "ln2_b",
        "lnc_w", "lnc_b", "b_q", "b_k", "b_v", "b_ctx"] + [f"ffb{c}" for c in range(FF)] + [f"fcb{c}" for c in range(FF)]
COL = {name: i for i, name in enumerate(VECS)}
ROWS = {name: i for i, name in enumerate(["sa_bo", "ca_bo", "ff_b2", "b_proj", "b_out", "b_fc2"])}
SQ = {name: i for i, name in enumerate(["q", "k", "v", "proj", "cq", "ck", "cv", "out", "ctx"])}
IDENT, COS, SIN, MASK = 0, P, 2 * P, 3 * P
COND = MASK + H
VEC = COND + B
NSMALL = VEC + len(VECS)
NMOD = 10

FILLS = ["q0", "k0", "q1", "k1", "v0", "v1"]


def build(nc, small_in, x_in, ctx_in, ctxT_in, wqkv_in, wo_in, wmod_in, wsq_in, wff_in, row_in, out):
    es = ExitStack()
    with es:
        def sb(name, shape, dt=F32):
            return es.enter_context(nc.sbuf_tensor(name, shape, dt))

        def sem(name):
            return es.enter_context(nc.semaphore(name))

        x = sb("x", [P, B, P])
        xn = sb("xn", [P, B, P])
        hT = sb("hT", [P, B * P])
        ctx = sb("ctx", [P, B, DC])
        ctxT = sb("ctxT", [DC, B * P])
        ctxnT = sb("ctxnT", [DC, B * P])
        hR = sb("hR", [P, 2, B * P], F32R)
        cR = sb("cR", [DC, 2, B * P], F32R)
        wR = sb("wR", [P, 2, 2, 2 * P], F32R)
        ctx1T = sb("ctx1T", [P, B * P])
        small = sb("small", [P, NSMALL])
        rows = sb("rows", [len(ROWS), P])
        rest = sb("rest", [len(ROWS), P])
        parts = sb("parts", [len(ROWS), 3, P], BF16)
        parts_row = sb("parts_row", [3, len(ROWS) * P], BF16)
        ones = sb("ones", [3, P], BF16)
        wmod = sb("wmod", [P, 10 * P])
        wsq = sb("wsq", [P, len(SQ) * P])
        wff = sb("wff", [P, 4 * FF * P])
        silu = sb("silu", [P, 4, B])
        idle = sb("idle", [P, BANK], BF16)
        primer = sb("primer", [P, 1])
        mod = sb("mod", [P, NMOD, B])
        bq_scaled = sb("bq_scaled", [P, 1])
        st = sb("st", [P, 2, B, 6])
        mv = sb("mv", [P, 2, B, 2])
        vare = sb("vare", [P, 2, B])
        neg_half = sb("neg_half", [P, B])
        rstd = sb("rstd", [P, 2, B])
        wqkv = sb("wqkv", [P, 2, 3 * P])
        wo = sb("wo", [P, 2, P])
        raw = sb("raw", [P, 4, BANK])
        swp = sb("swp", [P, 4, BANK])
        qk = sb("qk", [P, 2, 4, BANK])
        v0 = sb("v0", [P, 2, B * P])
        prob = sb("prob", [P, 4, BANK])
        probT = sb("probT", [P, 4, BANK])
        nmax = sb("nmax", [P, 4 * HALF])
        zsum = sb("zsum", [P, 4 * HALF])
        rz = sb("rz", [P, 4 * HALF])
        oT = sb("oT", [P, B * P])
        q1 = sb("q1", [P, B * P])
        k1 = sb("k1", [P, 2, B * P])
        v1 = sb("v1", [P, 2, B, P])
        km = sb("km", [P, 2, 2, B * P])
        vst = sb("vst", [P, 2, B, 2, VW])
        oS = sb("oS", [P, 2 * P])
        rzo = sb("rzo", [P, 2 * B])
        oN = sb("oN", [P, B, P])
        gT = sb("gT", [P, FF, B * P])

        bank = [es.enter_context(nc.psum_tensor(f"bank{i}", [P, BANK], F32)) for i in range(8)]
        ident = small[:, IDENT:IDENT + P]
        condT = small[:, COND:COND + B]
        cos = small[:, COS:COS + P].unsqueeze(1).broadcast_to([P, HALF, P])
        sin = small[:, SIN:SIN + P].unsqueeze(1).broadcast_to([P, HALF, P])

        def vcol(name, n=P):
            return small[0:n, VEC + COL[name]:VEC + COL[name] + 1]

        def four(ap):
            return ap.rearrange("p (u t) -> p u t", u=HALF)

        ld_x = [sem(f"ld_x{half}") for half in range(2)]
        ld_ctx, ld_ctxT, ld_small, ld_rows, ld_mod, ld_sq, ld_ff = (
            sem(f"ld_{s}") for s in ("ctx", "ctxT", "small", "rows", "mod", "sq", "ff"))
        ld_wqkv = [sem(f"ld_wqkv{p}") for p in range(2)]
        ld_wo = [sem(f"ld_wo{p}") for p in range(2)]
        dve_link = sem("dve_link")
        presets = sem("presets")
        padded = sem("padded")
        row_part = sem("row_part")
        row_moved = sem("row_moved")
        exp_c, silu_done, mod_ps, mod_done = sem("exp_c"), sem("silu_done"), sem("mod_ps"), sem("mod_done")
        ctx_mv, ctx_rstd, ctx_n, ctx_T, ctx_h = (sem(f"ctx_{s}") for s in ("mv", "rstd", "n", "T", "h"))
        ln_mv, ln_rstd, ln_xn, ln_T = (sem(f"ln_{s}") for s in ("mv", "rstd", "xn", "T"))
        ln_hA, ln_hD = sem("ln_hA"), sem("ln_hD")
        scores, rowmax, exps, recips, norms, probs_T, probs_Tc, pv, o_copied = (
            sem(s) for s in ("scores", "rowmax", "exps", "recips", "norms", "probs_T", "probs_Tc", "pv", "o_copied"))
        wo_done = sem("wo_done")
        filled, fill_out = [[sem(f"{s}_{f}") for f in FILLS] for s in ("filled", "fill_out")]
        swapped, rope_cos, rope_sin, roped = (
            [sem(f"{s}_{f}") for f in FILLS[:4]] for s in ("swapped", "rope_cos", "rope_sin", "roped"))
        act_high, act_low = sem("act_high"), sem("act_low")
        w_high, w_split = sem("w_high"), sem("w_split")
        acc_done = sem("acc_done")
        x_sum = sem("x_sum")
        x_done = sem("x_done")
        a_scores, a_rowmax, a_exps, a_T, a_pv, a_ev, a_back, a_rzo, a_norm, a_km, a_vst = (
            sem(f"a_{s}") for s in ("scores", "rowmax", "exps", "T", "pv", "ev", "back", "rzo", "norm", "km", "vst"))
        a_Tc = [sem("a_Tc_even"), sem("a_Tc_odd")]
        pre, pre_out = sem("pre"), sem("pre_out")
        end_ev, end_back, end_rzo, end_norm = (sem(f"end_{s}") for s in ("ev", "back", "rzo", "norm"))
        post_T, post_oT = sem("post_T"), sem("post_oT")
        ffn_h, ffn_g = sem("ffn_h"), sem("ffn_g")
        stored = sem("stored")

        PRE0 = [("ctx1", 0, 5), ("ctx1", 1, 5), ("ck", 0, 5), ("ck", 1, 5), ("cv", 0, 5), ("cv", 1, 5)]
        PRE1 = [("k", 0, 4), ("q", 0, 5), ("v", 0, 2), ("k", 1, 3), ("q", 1, 4), ("v", 1, 5)]
        PRE2 = [("cq", 0, 4), ("cq", 1, 5)]
        PRE = PRE0 + PRE1 + PRE2
        NPRE = [len(PRE0), len(PRE0) + len(PRE1), len(PRE)]
        MLP_BANKS = [4, 5, 2, 3]
        POOL_SUMS = (2, 3)
        END_O, END_BACK = (6, 0), (7, 1)
        FIRST_BANKS = [5, 4, 0, 1, 2, 3]
        LN_BANKS = [(2, 3), (0, 1)]
        MOD_STAGES = [(0, 2), (2, NMOD)]
        MOD_BANKS = [6, 7]
        CTX_BANKS = [6, 4]
        MODS = [0, 0, 2, 4, 6, 8]

        NOTHING = (None, None, None)

        def slots(n, is_last, a):
            if not is_last:
                return [("fill", n + 1, f) for f in range(6)]
            if a == 0:
                return [("fill", STEPS, 1), ("fill", STEPS, 3), NOTHING, NOTHING, ("fill", STEPS, 4), ("fill", STEPS, 5)]
            return [("pre", j, None) for j in range(len(PRE0))]

        def head_pairs(eng, first, step):
            step(first, first % 2, True, False)
            with eng.Fori(0, (STEPS - 2) // 2) as r:
                for p in range(2):
                    step(r * 2 + (first + 1 + p), (first + 1 + p) % 2, False, False)
            step(first + STEPS - 1, (first + STEPS - 1) % 2, False, True)

        block = es.enter_context(nc.Block())

        @block.sync
        def _(sp):
            for half in range(2):
                b0 = HALF * half
                sp.dma_start(x[:, b0:b0 + HALF, :], x_in[b0:b0 + HALF, :, :].rearrange("b t d -> t b d")).then_inc(
                    ld_x[half], 16)
            sp.dma_start(wqkv[:, 0, :], wqkv_in[0, :, :]).then_inc(ld_wqkv[0], 16)
            sp.dma_start(wqkv[:, 1, :], wqkv_in[1, :, :]).then_inc(ld_wqkv[1], 16)
            sp.dma_start(wo[:, 0, :], wo_in[0, :, :]).then_inc(ld_wo[0], 16)
            sp.dma_start(wo[:, 1, :], wo_in[1, :, :]).then_inc(ld_wo[1], 16)
            sp.dma_start(ctx[:, :, :], ctx_in.rearrange("b t d -> t b d")).then_inc(ld_ctx, 16)
            sp.dma_start(ctxT[:, :], ctxT_in).then_inc(ld_ctxT, 16)
            sp.dma_start(wsq[:, :], wsq_in).then_inc(ld_sq, 16)
            sp.dma_start(wff[:, :], wff_in).then_inc(ld_ff, 16)
            sp.wait_ge(row_part, 5)
            for j in range(3):
                sp.dma_start(parts_row[j:j + 1, :], parts[:, j, :]).then_inc(row_moved, 16)

            def swap(m, f):
                sp.wait_ge(fill_out[f], m + 1)
                if not (isinstance(m, int) and m == 0):
                    sp.wait_ge(roped[f], m)
                for e in range(2):
                    sp.dma_start(swp[e:P:2, f, :], raw[1 - e:P:2, f, :]).then_inc(swapped[f], 16)

            def load_wqkv(n, p):
                for f in range(6):
                    sp.wait_ge(filled[f], n + 1)
                sp.dma_start(wqkv[:, p, :], wqkv_in[bass.ds(n + 2, 1), :, :].rearrange("o p c -> p (o c)")).then_inc(
                    ld_wqkv[p], 16)

            def load_wo(n, p):
                sp.wait_ge(wo_done, n * 2)
                sp.dma_start(wo[:, 1 - p, :], wo_in[bass.ds(n + 1, 1), :, :].rearrange("o p c -> p (o c)")).then_inc(
                    ld_wo[1 - p], 16)

            def l0_step(n, p, is_first, is_last, a):
                if not (a == 1 and is_last):
                    load_wqkv(n, p)
                for kind, m, f in slots(n, is_last, a):
                    if kind == "fill" and f < 4:
                        swap(m, f)
                if not (a == 0 and is_first) and not (a == 1 and is_last):
                    load_wo(n, p)

            for a in range(2):
                for f in range(0, 4, 1 + a):
                    swap(STEPS * a, f)
                head_pairs(sp, STEPS * a, partial(l0_step, a=a))
            for half in range(2):
                b0 = HALF * half
                sp.wait_ge(x_done, half + 1)
                sp.dma_start(out[b0:b0 + HALF, :, :].rearrange("b t d -> t b d"), x[:, b0:b0 + HALF, :]).then_inc(
                    stored, 16)
            sp.wait_ge(stored, 32)

        @block.gpsimd
        def _(pool):
            pool.dma_start(rows[:, :], row_in).then_inc(ld_rows, 16)
            for p in range(2):
                for hh in range(2):
                    pool.memset(vst[:, p, :, hh, HW * (1 - hh):HW * (2 - hh)], 0.0).then_inc(padded, 1)
                    pool.memset(vst[:, p, :, hh, HW * hh + DH1:HW * hh + HW], 0.0).then_inc(padded, 1)
                pool.wait_ge(padded, 6 * p + 4)
                for hh in range(2):
                    pool.memset(vst[:, p, :, hh, HW * hh + DH1:HW * hh + DH1 + 1], 1.0).then_inc(padded, 1)

            def inv_std(k):
                for half in range(2):
                    cols = slice(HALF * half, HALF * (half + 1))
                    pool.wait_ge(ln_mv, 2 * k + half + 1)
                    nc.gpsimd.tensor_tensor(rstd[:, 0, cols], vare[:, 0, cols], neg_half[:, cols], ALU.pow).then_inc(
                        ln_rstd, 1)

            def rope_sum(m, f, mp):
                pool.wait_ge(rope_sin[f], m + 1)
                pool.wait_ge(rope_cos[f], m + 1)
                nc.gpsimd.tensor_tensor(qk[:, mp, f, :], qk[:, mp, f, :], swp[:, f, :], ALU.add).then_inc(roped[f], 1)

            def rope_sine(m, f):
                pool.wait_ge(swapped[f], m * 32 + 32)
                nc.gpsimd.tensor_tensor(four(swp[:, f, :]), four(swp[:, f, :]), sin, ALU.mult).then_inc(rope_sin[f], 1)

            def l0_step(n, p, is_first, is_last, a):
                todo = [(m, f) for kind, m, f in slots(n, is_last, a) if kind == "fill" and f < 4]
                for m, f in todo:
                    rope_sine(m, f)
                    if f == 0:
                        if is_first:
                            low_part(hR, hT, 2 * a, 0)
                        split_weights(n, p, a)
                for m, f in todo:
                    if f in POOL_SUMS:
                        rope_sum(m, f, 1 - p)
                if is_first:
                    low_part(hR, hT, 2 * a, 1)

            def low_part(dst, src, before, half):
                pool.wait_ge(act_high, before + 1)
                cols = slice(half * BANK, (half + 1) * BANK)
                nc.gpsimd.tensor_tensor(dst[:, 1, cols], src[:, cols], dst[:, 0, cols].bitcast(F32), ALU.subtract).then_inc(
                    act_low, 1)

            def split_weights(n, p, a):
                pool.wait_ge(w_high, n + (1 - a))
                nc.gpsimd.tensor_tensor(wR[:, p, 1, :], wqkv[:, p, 0:2 * P], wR[:, p, 0, :].bitcast(F32),
                                        ALU.subtract).then_inc(w_split, 1)

            def split_rows():
                pool.wait_ge(ld_rows, 16)
                src, done = rows, 0
                for j in range(3):
                    nc.gpsimd.tensor_copy(parts[:, j, :], src[:, :]).then_inc(row_part, 1)
                    done += 1
                    pool.wait_ge(row_part, done)
                    if j < 2:
                        nc.gpsimd.tensor_tensor(rest[:, :], src[:, :], parts[:, j, :], ALU.subtract).then_inc(row_part, 1)
                        done += 1
                        pool.wait_ge(row_part, done)
                        src = rest

            def stage_values(m, p, a):
                pool.wait_ge(padded, 12)
                if not (isinstance(m, int) and m < 2):
                    pool.wait_ge(a_pv, m * 4 - 4)
                src = v1[:, a, :, bass.ds(m * (2 * DH1) - a * P, 2 * DH1)].rearrange("p b (h d) -> p b h d", h=2)
                dst = vst[:, p, :, :, :].rearrange("p b h w -> p b (h w)")
                for hh in range(2):
                    ins = nc.gpsimd.tensor_copy(dst[:, :, (VW + HW) * hh:(VW + HW) * hh + DH1], src[:, :, hh, :])
                ins.then_inc(a_vst, 1)

            def l1_step(n, p, is_first, is_last, a):
                if not is_last:
                    stage_values(n + 1, 1 - p, a)

            inv_std(0)
            split_rows()
            pool.wait_ge(ctx_mv, 1)
            nc.gpsimd.tensor_tensor(rstd[:, 1, :], vare[:, 1, :], neg_half[:, :], ALU.pow).then_inc(ctx_rstd, 1)
            for a in range(2):
                if a:
                    inv_std(1)
                    for half in range(2):
                        low_part(cR, ctxnT, 1, half)
                for f in range(0, 4, 1 + a):
                    rope_sine(STEPS * a, f)
                head_pairs(pool, STEPS * a, partial(l0_step, a=a))
            inv_std(2)
            for a in range(2):
                if a == 0:
                    inv_std(3)
                    pool.wait_ge(pre_out, NPRE[1])
                stage_values(STEPS * a, 0, a)
                if a:
                    inv_std(4)
                head_pairs(pool, STEPS * a, partial(l1_step, a=a))
            inv_std(5)

        @block.scalar
        def _(act):
            act.dma_start(small[:, :], small_in).then_inc(ld_small, 16)
            act.dma_start(wmod[:, :], wmod_in).then_inc(ld_mod, 16)
            act.wait_ge(ld_small, 16)
            nc.scalar.activation(silu[:, 0, :], condT, ACT.Exp, scale=-1.0).then_inc(exp_c, 1)

            def load_table(func):
                nc.scalar.activation(primer[:, :], small[:, 0:1], func)

            def ln_scale_shift(k, half):
                if k < 2 and half == 0:
                    act.wait_ge(mod_done, k + 1)
                j = MODS[k]
                for e in range(2 - half):
                    act.wait_ge(ln_T, 4 * k + 2 * half + e + 1)
                    for u in range(2):
                        b = HALF * half + 2 * e + u
                        last = nc.scalar.activation(hT[:, b * P:(b + 1) * P], bank[LN_BANKS[half][e]][:, u * P:(u + 1) * P],
                                                    ACT.Identity, bias=mod[:, j + 1, b:b + 1], scale=mod[:, j, b:b + 1])
                last.then_inc(ln_hA, 1)

            def evacuate_fill(m, f, mp, src=5):
                act.wait_ge(filled[f], m + 1)
                if f < 4:
                    if not (isinstance(m, int) and m == 0):
                        act.wait_ge(swapped[f], m * 32)
                        act.wait_ge(rope_cos[f], m)
                    ins = nc.scalar.activation(raw[:, f, :], bank[src][:, :], ACT.Copy,
                                               scale=DH0 ** -0.5 if f in (0, 2) else 1.0)
                else:
                    ins = nc.scalar.activation(v0[:, mp, (f - 4) * BANK:(f - 3) * BANK], bank[src][:, :], ACT.Copy)
                ins.then_inc(fill_out[f], 1)

            def exp0(n, g):
                act.wait_ge(rowmax, n * 4 + (g + 1))
                for u in range(HALF):
                    c = g * HALF + u
                    last = nc.scalar.activation(prob[:, g, u * P:(u + 1) * P], bank[g % 2][:, u * P:(u + 1) * P],
                                                ACT.Exp, bias=nmax[:, c:c + 1], accum_out=zsum[:, c:c + 1])
                last.then_inc(exps, 1)

            def weights_high(n, p):
                act.wait_ge(ld_wqkv[p], n * 8 + (32 - 8 * p))
                act.wait_ge(filled[3], n + 1)
                nc.scalar.activation(wR[:, p, 0, :], wqkv[:, p, 0:2 * P], ACT.Copy).then_inc(w_high, 1)

            def high_part(dst, src, done):
                nc.scalar.activation(dst[:, 0, :], src[:, :], ACT.Copy).then_inc(act_high, 1)

            def evacuate_o(n, half):
                act.wait_ge(pv, n * 2 + (half + 1))
                nc.scalar.activation(oT[:, half * BANK:(half + 1) * BANK], bank[4][:, :], ACT.Copy).then_inc(o_copied, 1)

            def l0_step(n, p, is_first, is_last, a):
                todo = slots(n, is_last, a)

                def slot(k):
                    kind, m, f = todo[k]
                    if kind == "fill":
                        evacuate_fill(m, f, 1 - p)
                    elif kind == "pre":
                        pre_evacuate(m)

                slot(0)
                if is_first:
                    high_part(hR, hT, 2 * a)
                exp0(n, 0)
                exp0(n, 1)
                slot(1)
                if is_first and a == 0:
                    act.wait_ge(ctx_T, 1)
                    nc.scalar.activation(ctxnT[:, 0:BANK], bank[CTX_BANKS[0]][0:DC, :], ACT.Identity,
                                         bias=vcol("lnc_b", DC), scale=vcol("lnc_w", DC)).then_inc(ctx_h, 1)
                if not is_first:
                    evacuate_o(n - 1, 1)
                if not is_last:
                    weights_high(n, p)
                slot(2)
                exp0(n, 2)
                slot(3)
                exp0(n, 3)
                slot(4)
                if not is_last:
                    slot(5)
                evacuate_o(n, 0)
                if is_last:
                    slot(5)
                    evacuate_o(n, 1)
                    if a == 0:
                        high_part(cR, ctxnT, 1)

            def pre_evacuate(j):
                what, half, ps = PRE[j]
                act.wait_ge(pre, j + 1)
                src = bank[ps][:, :]
                cols = slice(half * BANK, (half + 1) * BANK)
                if what == "ctx1":
                    ins = nc.scalar.activation(ctx1T[:, cols], src, ACT.Identity, bias=vcol("b_ctx"))
                elif what == "q":
                    ins = nc.scalar.activation(q1[:, cols], src, ACT.Identity, bias=bq_scaled[:, :], scale=DH1 ** -0.5)
                elif what == "cq":
                    ins = nc.scalar.activation(q1[:, cols], src, ACT.Copy, scale=DH1 ** -0.5)
                elif what == "k":
                    ins = nc.scalar.activation(k1[:, 0, cols], src, ACT.Identity, bias=vcol("b_k"))
                elif what == "ck":
                    ins = nc.scalar.activation(k1[:, 1, cols], src, ACT.Copy)
                else:
                    a = 0 if what == "v" else 1
                    ins = nc.scalar.activation(v1[:, a, HALF * half:HALF * (half + 1), :], four(src), ACT.Copy)
                ins.then_inc(pre_out, 1)

            def gelu(k, func, bias):
                base = 0 if k == 2 else 2 * FF
                ln_scale_shift(k, 0)
                for j in range(2 * FF):
                    c, half = j % FF, j // FF
                    if j == 2:
                        ln_scale_shift(k, 1)
                    act.wait_ge(ffn_h, base + j + 1)
                    nc.scalar.activation(gT[:, c, half * BANK:(half + 1) * BANK], bank[MLP_BANKS[j % 4]][:, :], func,
                                         bias=vcol(f"{bias}{c}")).then_inc(ffn_g, 1)

            def exp1(n, g):
                act.wait_ge(a_rowmax, n * 4 + (g + 1))
                for u in range(HALF):
                    c = g * HALF + u
                    last = nc.scalar.activation(prob[:, g, u * P:(u + 1) * P], bank[g][:, u * P:(u + 1) * P],
                                                ACT.Exp, bias=nmax[:, c:c + 1])
                last.then_inc(a_exps, 1)

            def copy_T(n, g):
                act.wait_ge(a_T, n * 4 + (g + 1))
                nc.scalar.activation(probT[:, g, :], bank[4 + g % 2][:, :], ACT.Copy).then_inc(a_Tc[1], 1)

            def evacuate_o1(n):
                act.wait_ge(a_pv, n * 4 + 4)
                nc.scalar.activation(oS[:, :], bank[6][:, 0:2 * P], ACT.Copy).then_inc(a_ev, 1)

            def evacuate_o1_half(n, a, half):
                if half == 0:
                    act.wait_ge(a_back, n)
                act.wait_ge(a_pv, n * 4 + (2 * half + 2))
                cols = slice(P * half, P * (half + 1))
                nc.scalar.activation(oS[:, cols], bank[END_O[half]][:, cols], ACT.Copy).then_inc(
                    a_ev if half else end_ev, 1)

            def l1_step(n, p, is_first, is_last, a):
                if is_first:
                    exp1(n, 0)
                else:
                    copy_T(n - 1, 3)
                exp1(n, 1)
                if not is_first:
                    evacuate_o1(n - 1)
                exp1(n, 2)
                copy_T(n, 1)
                exp1(n, 3)
                if not is_last:
                    exp1(n + 1, 0)
                else:
                    evacuate_o1_half(n, a, 0)
                    copy_T(n, 3)
                    evacuate_o1_half(n, a, 1)

            def evacuate_post(a):
                for half in range(2):
                    act.wait_ge(post_T, 2 * a + half + 1)
                    dst, src = oT[:, half * BANK:(half + 1) * BANK], bank[4 + half][:, :]
                    if a == 0:
                        ins = nc.scalar.activation(dst, src, ACT.Identity, bias=vcol("b_v"))
                    else:
                        ins = nc.scalar.activation(dst, src, ACT.Copy)
                    ins.then_inc(post_oT, 1)

            for a in range(2):
                ln_scale_shift(a, 0)
                for f in (range(6) if a == 0 else (0, 2)):
                    if f == 2:
                        ln_scale_shift(a, 1)
                    evacuate_fill(STEPS * a, f, 0, FIRST_BANKS[f])
                head_pairs(act, STEPS * a, partial(l0_step, a=a))
            load_table(ACT.Gelu)
            gelu(2, ACT.Gelu, "ffb")
            load_table(ACT.Exp)
            for a in range(2):
                ln_scale_shift(3 + a, 0)
                for j in range(NPRE[a], NPRE[a + 1]):
                    if PRE[j][1] and not PRE[j - 1][1]:
                        ln_scale_shift(3 + a, 1)
                    pre_evacuate(j)
                head_pairs(act, STEPS * a, partial(l1_step, a=a))
                evacuate_post(a)
            load_table(ACT.Gelu_apprx_tanh)
            gelu(5, ACT.Gelu_apprx_tanh, "fcb")

        @block.vector
        def _(dve):
            links = [0]

            def link(ins):
                links[0] += 1
                ins.then_inc(dve_link, 1)
                dve.wait_ge(dve_link, links[0])

            nc.vector.memset(idle[:, :], 0.0).then_inc(presets, 1)
            nc.vector.memset(ones[:, :], 1.0).then_inc(presets, 1)
            nc.vector.memset(neg_half[:, :], -0.5)

            def statistics(c, src, b0, b1, eps):
                for b in range(b0, b1):
                    last = nc.vector.bn_stats(st[:, c, b, :], src[:, b, :])
                link(last)
                for b in range(b0, b1):
                    last = nc.vector.bn_aggr(mv[:, c, b, :], st[:, c, b, :])
                link(last)
                return nc.vector.tensor_scalar(vare[:, c, b0:b1], mv[:, c, b0:b1, 1], eps, None, ALU.add)

            def ln_stats(k, half):
                statistics(0, x, HALF * half, HALF * (half + 1), EPS0 if k < 3 else EPS1).then_inc(ln_mv, 1)

            def ln_normalise(k, half):
                if k and half == 0:
                    dve.wait_ge(ln_T, 4 * k)
                dve.wait_ge(ln_rstd, 2 * k + half + 1)
                for b in range(HALF * half, HALF * (half + 1)):
                    ins = nc.vector.tensor_scalar(xn[:, b, :], x[:, b, :], mv[:, 0, b, 0:1], rstd[:, 0, b:b + 1],
                                                  ALU.subtract, ALU.mult)
                    if b % 2:
                        ins.then_inc(ln_xn, 1)

            def ln_scale_shift(k):
                dve.wait_ge(ln_T, 4 * k + 4)
                ps, b0, j = bank[LN_BANKS[1][1]], HALF + 2, MODS[k]
                for u in range(2):
                    b = b0 + u
                    last = nc.vector.tensor_scalar(hT[:, b * P:(b + 1) * P], ps[:, u * P:(u + 1) * P],
                                                   mod[:, j, b:b + 1], mod[:, j + 1, b:b + 1], ALU.mult, ALU.add)
                last.then_inc(ln_hD, 1)

            def context_norm():
                dve.wait_ge(ctx_rstd, 1)
                for b in range(B):
                    last = nc.vector.tensor_scalar(ctx[:, b, :], ctx[:, b, :], mv[:, 1, b, 0:1], rstd[:, 1, b:b + 1],
                                                   ALU.subtract, ALU.mult)
                last.then_inc(ctx_n, 1)

            def residual(half, sublayer):
                xs = x[:, HALF * half:HALF * (half + 1), :]
                if sublayer < 2:
                    dve.wait_ge(wo_done, 2 * STEPS * (sublayer + 1) - 1 + half)
                else:
                    dve.wait_ge(acc_done, 2 * (sublayer - 2) + half + 1)
                ins = nc.vector.tensor_tensor(xs, xs, four(bank[6 + half][:, :]), ALU.add)
                if sublayer == 5:
                    ins.then_inc(x_done, 1)
                else:
                    ins.then_inc(x_sum, 1)
                    dve.wait_ge(x_sum, 2 * sublayer + half + 1)

            def layer_norm(k, begun, meanwhile=None):
                if not begun:
                    residual(0, k - 1)
                    ln_stats(k, 0)
                if meanwhile:
                    meanwhile()
                ln_normalise(k, 0)
                residual(1, k - 1)
                ln_stats(k, 1)
                ln_normalise(k, 1)
                ln_scale_shift(k)

            def silu_condition():
                dve.wait_ge(exp_c, 1)
                link(nc.vector.tensor_scalar(silu[:, 1, :], silu[:, 0, :], 1.0, None, ALU.add))
                link(nc.vector.reciprocal(silu[:, 2, :], silu[:, 1, :]))
                nc.vector.tensor_tensor(silu[:, 3, :], silu[:, 2, :], condT, ALU.mult).then_inc(silu_done, 1)

            def modulation(stage):
                (j0, j1), ln = MOD_STAGES[stage], ("ln1", "ln2")[stage]
                dve.wait_ge(mod_ps, stage + 1)
                bias = small[:, VEC + j0:VEC + j1].unsqueeze(2).broadcast_to([P, j1 - j0, B])
                products = bank[MOD_BANKS[stage]][:, 0:(j1 - j0) * B].rearrange("p (j b) -> p j b", b=B)
                link(nc.vector.tensor_tensor(mod[:, j0:j1, :], products, bias, ALU.add))
                link(nc.vector.tensor_scalar(mod[:, j0:j1:2, :], mod[:, j0:j1:2, :], 1.0, None, ALU.add))
                link(nc.vector.scalar_tensor_tensor(mod[:, j0 + 1, :], mod[:, j0, :], vcol(f"{ln}_b"), mod[:, j0 + 1, :],
                                                    ALU.mult, ALU.add))
                link(nc.vector.tensor_scalar(mod[:, j0, :], mod[:, j0, :], vcol(f"{ln}_w"), None, ALU.mult))
                nc.vector.engine_nop().then_inc(mod_done, 1)

            def row_max(n, g):
                dve.wait_ge(scores, n * 4 + (g + 1))
                nc.vector.tensor_reduce(nmax[:, g * HALF:(g + 1) * HALF], four(bank[g % 2][:, :]), AX.X, ALU.max,
                                        negate=True).then_inc(rowmax, 1)

            def normalise(n, g):
                dve.wait_ge(exps, n * 4 + (g + 1))
                cols = slice(g * HALF, (g + 1) * HALF)
                nc.vector.reciprocal(rz[:, cols], zsum[:, cols]).then_inc(recips, 1)
                dve.wait_ge(recips, n * 4 + (g + 1))
                nc.vector.tensor_tensor(four(prob[:, g, :]), four(prob[:, g, :]),
                                        rz[:, cols].unsqueeze(2).broadcast_to([P, HALF, P]), ALU.mult).then_inc(norms, 1)

            def copy_T0(n, g):
                dve.wait_ge(probs_T, n * 4 + (g + 1))
                nc.vector.tensor_copy(probT[:, g, :], bank[2 + g % 2][:, :]).then_inc(probs_Tc, 1)

            def rope_cosine(m, f, mp):
                dve.wait_ge(fill_out[f], m + 1)
                nc.vector.tensor_tensor(four(qk[:, mp, f, :]), four(raw[:, f, :]), cos, ALU.mult).then_inc(rope_cos[f], 1)

            def rope_sum(m, f, mp):
                dve.wait_ge(rope_sin[f], m + 1)
                dve.wait_ge(rope_cos[f], m + 1)
                nc.vector.tensor_tensor(qk[:, mp, f, :], qk[:, mp, f, :], swp[:, f, :], ALU.add).then_inc(roped[f], 1)

            def l0_step(n, p, is_first, is_last, a):
                todo = [(m, f) for kind, m, f in slots(n, is_last, a) if kind == "fill" and f < 4]

                def cosine(k):
                    if k < len(todo):
                        rope_cosine(*todo[k], 1 - p)

                def total(k):
                    if k < len(todo) and todo[k][1] not in POOL_SUMS:
                        rope_sum(*todo[k], 1 - p)

                row_max(n, 0)
                row_max(n, 1)
                if is_first:
                    for f in ((2, 3) if a == 0 else (2,)):
                        rope_sum(n, f, 0)
                cosine(0)
                normalise(n, 0)
                row_max(n, 2)
                if is_first and a == 0:
                    dve.wait_ge(ctx_T, 2)
                    nc.vector.tensor_scalar(ctxnT[:, BANK:2 * BANK], bank[CTX_BANKS[1]][0:DC, :], vcol("lnc_w", DC),
                                            vcol("lnc_b", DC), ALU.mult, ALU.add).then_inc(ctx_h, 1)
                normalise(n, 1)
                total(0)
                cosine(1)
                cosine(2)
                row_max(n, 3)
                copy_T0(n, 0)
                copy_T0(n, 1)
                if is_first and a == 0:
                    modulation(1)
                normalise(n, 2)
                normalise(n, 3)
                total(1)
                cosine(3)
                copy_T0(n, 2)
                copy_T0(n, 3)
                if is_last:
                    residual(0, a)
                    ln_stats(a + 1, 0)

            def mask_keys(m, p, a, hh):
                nc.vector.tensor_scalar(km[:, p, hh, :], k1[:, a, :], small[:, bass.ds(m * 2 + (MASK + hh - a * H), 1)],
                                        None, ALU.mult).then_inc(a_km, 1)

            def row_max1(n, g):
                dve.wait_ge(a_scores, n * 4 + (g + 1))
                nc.vector.tensor_reduce(nmax[:, g * HALF:(g + 1) * HALF], four(bank[g][:, :]), AX.X, ALU.max,
                                        negate=True).then_inc(a_rowmax, 1)

            def copy_T1(n, g):
                dve.wait_ge(a_T, n * 4 + (g + 1))
                nc.vector.tensor_copy(probT[:, g, :], bank[4 + g % 2][:, :]).then_inc(a_Tc[0], 1)

            def divide(n, a):
                dve.wait_ge(a_back, n + 1)
                src = bank[7][:, 0:2 * P].rearrange("p (b h v) -> p b h v", b=B, h=2)
                recip = rzo[:, :].rearrange("p (b h) -> p b h", b=B)
                nc.vector.reciprocal(recip, src[:, :, :, DH1]).then_inc(a_rzo, 1)
                dve.wait_ge(a_rzo, n + 1)
                dst = oN[:, :, bass.ds(n * (2 * DH1) - a * P, 2 * DH1)].rearrange("p b (h d) -> p b h d", h=2)
                nc.vector.tensor_tensor(dst, src[:, :, :, 0:DH1], recip.unsqueeze(3).broadcast_to([P, B, 2, DH1]),
                                        ALU.mult).then_inc(a_norm, 1)

            def divide_half(n, a, half):
                back, recip, norm, count = (a_back, a_rzo, a_norm, n + 1) if half else (end_back, end_rzo, end_norm, a + 1)
                hb = slice(HALF * half, HALF * (half + 1))
                dve.wait_ge(back, count)
                src = bank[END_BACK[half]][:, 0:2 * P].rearrange("p (b h v) -> p b h v", b=B, h=2)[:, hb, :, :]
                rz_half = rzo[:, :].rearrange("p (b h) -> p b h", b=B)[:, hb, :]
                nc.vector.reciprocal(rz_half, src[:, :, :, DH1]).then_inc(recip, 1)
                dve.wait_ge(recip, count)
                dst = oN[:, hb, (n - STEPS * a) * 2 * DH1:(n - STEPS * a + 1) * 2 * DH1].rearrange(
                    "p b (h d) -> p b h d", h=2)
                nc.vector.tensor_tensor(dst, src[:, :, :, 0:DH1], rz_half.unsqueeze(3).broadcast_to([P, HALF, 2, DH1]),
                                        ALU.mult).then_inc(norm, 1)

            def l1_step(n, p, is_first, is_last, a):
                if is_first:
                    for g in range(3):
                        row_max1(n, g)
                if not is_last:
                    mask_keys(n + 1, 1 - p, a, 0)
                row_max1(n, 3)
                if not is_last:
                    mask_keys(n + 1, 1 - p, a, 1)
                copy_T1(n, 0)
                if not is_last:
                    row_max1(n + 1, 0)
                    row_max1(n + 1, 1)
                copy_T1(n, 2)
                if not is_first:
                    divide(n - 1, a)
                if not is_last:
                    row_max1(n + 1, 2)
                else:
                    for half in range(2):
                        divide_half(n, a, half)

            dve.wait_ge(ld_small, 16)
            silu_condition()
            nc.vector.tensor_scalar(bq_scaled[:, :], vcol("b_q"), DH1 ** -0.5, None, ALU.mult)
            dve.wait_ge(ld_x[0], 16)
            ln_stats(0, 0)
            dve.wait_ge(ld_x[1], 16)
            ln_stats(0, 1)
            ln_normalise(0, 0)
            modulation(0)
            ln_normalise(0, 1)
            dve.wait_ge(ld_ctx, 16)
            statistics(1, ctx, 0, B, EPS0).then_inc(ctx_mv, 1)
            ln_scale_shift(0)
            for a in range(2):
                if a:
                    layer_norm(1, True)
                for f in range(0, 4, 1 + a):
                    rope_cosine(STEPS * a, f, 0)
                for f in ((0, 1) if a == 0 else (0,)):
                    rope_sum(STEPS * a, f, 0)
                if a == 0:
                    context_norm()
                head_pairs(dve, STEPS * a, partial(l0_step, a=a))
            layer_norm(2, True)
            for a in range(2):
                if a == 0:
                    layer_norm(3, False)
                    dve.wait_ge(pre_out, NPRE[0] + 4)
                    mask_keys(0, 0, 0, 0)
                else:
                    layer_norm(4, False, partial(mask_keys, STEPS, 0, 1, 0))
                mask_keys(STEPS * a, 0, a, 1)
                head_pairs(dve, STEPS * a, partial(l1_step, a=a))
            layer_norm(5, False)
            for half in range(2):
                residual(half, 5)

        @block.tensor
        def _(pe):
            def mm(o, lhsT, rhs, start, stop):
                return nc.tensor.matmul(o, lhsT, rhs, start=start, stop=stop, skip_group_check=True)

            def bcols(b):
                return slice(b * P, (b + 1) * P)

            def transpose_norm(k, half):
                if k:
                    pe.wait_ge(ln_hA, 2 * k + half - 1)
                    if half:
                        pe.wait_ge(ln_hD, k)
                for e in range(2):
                    pe.wait_ge(ln_xn, 4 * k + 2 * half + e + 1)
                    for u in range(2):
                        last = nc.tensor.transpose(bank[LN_BANKS[half][e]][:, bcols(u)],
                                                   xn[:, HALF * half + 2 * e + u, :], ident)
                    last.then_inc(ln_T, 1)

            def keep_warm(count, ps):
                for _ in range(count):
                    mm(bank[ps][:, :], idle[:, 0:P], idle[:, :], True, True)

            def wait_hT(k, half):
                pe.wait_ge(ln_hA, 2 * k + half + 1)
                if half:
                    pe.wait_ge(ln_hD, k + 1)

            def seed(name, half):
                pe.wait_ge(row_moved, 48)
                cols = slice(ROWS[name] * P, (ROWS[name] + 1) * P)
                mm(four(bank[6 + half][:, :]), ones[:, :],
                   parts_row[:, cols].unsqueeze(1).broadcast_to([3, HALF, P]), start=True, stop=False)

            def fill(m, f, mp, a, k=None, ps=5, after=None, high_low=False):
                kv, width = (hT, P) if a == 0 else (ctxnT, DC)
                half = f - 4 if f > 3 else f // 2
                if k is not None:
                    wait_hT(k, half)
                pe.wait_ge(ld_wqkv[mp], m * 8 + (16 - 8 * mp))
                if after is not None:
                    pe.wait_ge(fill_out[after[1]], after[0] + 1)
                cols = slice(half * BANK, (half + 1) * BANK)
                if high_low and f < 4:
                    src, lanes, w0 = (cR, DC, P) if a and f in (1, 3) else (hR, P, P * (f % 2))
                    if f == 0:
                        pe.wait_ge(w_split, m - 1 - a)
                    if f in (0, 2):
                        pe.wait_ge(act_low, 4 * a + 1 + half)
                    for j, (i, o) in enumerate(((0, 0), (0, 1), (1, 0))):
                        last = mm(bank[ps][:, :], wR[0:lanes, mp, i, w0:w0 + P], src[:, o, cols], j == 0, j == 2)
                elif f in (0, 2):
                    last = mm(bank[ps][:, :], wqkv[:, mp, 0:P], hT[:, cols], True, True)
                elif f in (1, 3):
                    last = mm(bank[ps][:, :], wqkv[0:width, mp, P:2 * P], kv[:, cols], True, True)
                else:
                    for u in range(HALF):
                        last = mm(bank[ps][:, bcols(u)], kv[:, bcols(HALF * half + u)], wqkv[0:width, mp, 2 * P:3 * P],
                                  True, True)
                last.then_inc(filled[f], 1)

            def score(n, p, g, lead):
                hh, half = g % 2, g // 2
                pe.wait_ge(roped[2 * half], n + 1)
                pe.wait_ge(roped[2 * half + 1], n + 1)
                if lead:
                    pe.wait_ge(fill_out[2 + g], n + 1)
                else:
                    pe.wait_ge(exps, n * 4 + (g - 1))
                lanes = slice(DH0 * hh, DH0 * (hh + 1))
                for u in range(HALF):
                    last = mm(bank[g % 2][:, bcols(u)], qk[lanes, p, 2 * half, bcols(u)],
                              qk[lanes, p, 2 * half + 1, bcols(u)], True, True)
                last.then_inc(scores, 1)

            def transpose_probs(n, g, is_first):
                pe.wait_ge(norms, n * 4 + (g + 1))
                if g >= 2 or not is_first:
                    pe.wait_ge(probs_Tc, n * 4 + (g - 1))
                else:
                    pe.wait_ge(fill_out[4 + g], n + 1)
                for u in range(HALF):
                    last = nc.tensor.transpose(bank[2 + g % 2][:, bcols(u)], prob[:, g, bcols(u)], ident)
                last.then_inc(probs_T, 1)

            def prob_values(n, p, half, is_first):
                pe.wait_ge(probs_Tc, n * 4 + (2 * half + 2))
                pe.wait_ge(fill_out[4 + half], n + 1)
                if half or not is_first:
                    pe.wait_ge(o_copied, n * 2 + half)
                else:
                    pe.wait_ge(ctx_h, 2)
                for u in range(HALF):
                    for hh in range(2):
                        b = HALF * half + u
                        last = mm(bank[4][DH0 * hh:DH0 * (hh + 1), bcols(u)],
                                  v0[:, p, b * P + DH0 * hh:b * P + DH0 * (hh + 1)], probT[:, 2 * half + hh, bcols(u)],
                                  True, True)
                last.then_inc(pv, 1)

            def project_out(n, p, half):
                pe.wait_ge(o_copied, n * 2 + (half + 1))
                if half == 0:
                    pe.wait_ge(ld_wo[p], n * 8 + (16 - 8 * p))
                for u in range(HALF):
                    last = mm(bank[6 + half][:, bcols(u)], oT[:, bcols(HALF * half + u)], wo[:, p, :], False, False)
                last.then_inc(wo_done, 1)

            def l0_step(n, p, is_first, is_last, a):
                todo = slots(n, is_last, a)

                def slot(k):
                    kind, m, f = todo[k]
                    if kind == "fill":
                        before = [g for other, _, g in todo[:k] if other]
                        fill(m, f, 1 - p, a if not is_last else 1, after=(m, before[-1]) if before else (n, 5),
                             high_low=not is_first and not is_last)
                    elif kind == "pre":
                        pre_fill(m)

                if is_first and a:
                    pe.wait_ge(x_sum, 2)
                    seed("ca_bo", 0)
                    seed("ca_bo", 1)
                if is_first:
                    slot(0)
                    if a:
                        keep_warm(4, 4)
                score(n, p, 0, is_first)
                if not is_first:
                    slot(0)
                score(n, p, 1, is_first)
                if not is_first:
                    project_out(n - 1, 1 - p, 0)
                slot(1)
                if is_first and a == 0:
                    pe.wait_ge(ctx_n, 1)
                    for half in range(2):
                        for u in range(HALF):
                            last = nc.tensor.transpose(bank[CTX_BANKS[half]][0:DC, bcols(u)], ctx[:, HALF * half + u, :],
                                                       ident)
                        last.then_inc(ctx_T, 1)
                if is_first and a:
                    keep_warm(5, 4)
                score(n, p, 2, False)
                if not is_first:
                    prob_values(n - 1, 1 - p, 1, False)
                slot(2)
                score(n, p, 3, False)
                transpose_probs(n, 0, is_first)
                slot(3)
                transpose_probs(n, 1, is_first)
                if not is_first:
                    project_out(n - 1, 1 - p, 1)
                slot(4)
                prob_values(n, p, 0, is_first)
                if not is_last:
                    slot(5)
                transpose_probs(n, 2, is_first)
                if is_last:
                    project_out(n, p, 0)
                transpose_probs(n, 3, is_first)
                if is_last:
                    slot(5)
                if is_first and a == 0:
                    pe.wait_ge(mod_done, 2)
                    pe.wait_ge(ctx_h, 2)
                    seed("sa_bo", 0)
                    seed("sa_bo", 1)
                if is_last:
                    prob_values(n, p, 1, False)
                    keep_warm(4, 0)
                    project_out(n, p, 1)
                    keep_warm(4, 0)

            def pre_fill(j):
                what, half, ps = PRE[j]
                same = [i for i in range(j) if PRE[i][2] == ps]
                if same:
                    pe.wait_ge(pre_out, same[-1] + 1)
                if j == 0:
                    pe.wait_ge(ld_sq, 16)
                    pe.wait_ge(ld_ctxT, 16)
                    pe.wait_ge(fill_out[5], 2 * STEPS)
                if what in ("ck", "cv"):
                    pe.wait_ge(pre_out, half + 1)
                if what in ("q", "k", "v"):
                    wait_hT(3, half)
                if what == "cq":
                    wait_hT(4, half)
                w = wsq[0:DC if what == "ctx1" else P, SQ["ctx" if what == "ctx1" else what] * P:][:, 0:P]
                src = {"ctx1": ctxT, "ck": ctx1T, "cv": ctx1T}.get(what, hT)
                if what in ("v", "cv"):
                    for u in range(HALF):
                        last = mm(bank[ps][:, bcols(u)], src[:, bcols(HALF * half + u)], w, True, True)
                else:
                    last = mm(bank[ps][:, :], w, src[:, half * BANK:(half + 1) * BANK], True, True)
                last.then_inc(pre, 1)

            def score1(n, p, g, lead):
                hh, half = g % 2, g // 2
                pe.wait_ge(a_km, n * 2 + (hh + 1))
                if not lead:
                    pe.wait_ge(a_exps, n * 4 + (g - 3))
                for u in range(HALF):
                    b = HALF * half + u
                    last = mm(bank[g][:, bcols(u)], q1[:, bcols(b)], km[:, p, hh, bcols(b)], True, True)
                last.then_inc(a_scores, 1)

            def transpose1(n, g, lead):
                pe.wait_ge(a_exps, n * 4 + (g + 1))
                if g >= 2:
                    pe.wait_ge(a_Tc[g % 2], n * 2 + (g // 2))
                elif not lead:
                    pe.wait_ge(a_Tc[g % 2], n * 2)
                for u in range(HALF):
                    last = nc.tensor.transpose(bank[4 + g % 2][:, bcols(u)], prob[:, g, bcols(u)], ident)
                last.then_inc(a_T, 1)

            def prob_values1(n, p, g, lead, ps=6):
                hh, half = g % 2, g // 2
                pe.wait_ge(a_Tc[g % 2], n * 2 + (g // 2 + 1))
                if g == 0:
                    pe.wait_ge(a_vst, n + 1)
                    if not lead:
                        pe.wait_ge(a_ev, n)
                for u in range(HALF):
                    last = mm(bank[ps][VW * u:VW * (u + 1), bcols(half)], vst[:, p, HALF * half + u, hh, :],
                              probT[:, g, bcols(u)], hh == 0, hh == 1)
                last.then_inc(a_pv, 1)

            def turn_back(n, lead):
                pe.wait_ge(a_ev, n + 1)
                if not lead:
                    pe.wait_ge(a_norm, n)
                for half in range(2):
                    last = nc.tensor.transpose(bank[7][:, bcols(half)], oS[:, bcols(half)], ident)
                last.then_inc(a_back, 1)

            def l1_step(n, p, is_first, is_last, a):
                lead = is_first and a == 0
                if is_first:
                    pe.wait_ge(pre_out, NPRE[a] + (1 if a else 2))
                    for g in range(3):
                        if g == 2:
                            pe.wait_ge(pre_out, NPRE[a + 1])
                        score1(n, p, g, lead)
                score1(n, p, 3, lead)
                transpose1(n, 0, lead)
                if not is_first:
                    prob_values1(n - 1, 1 - p, 3, False)
                if not is_last:
                    score1(n + 1, 1 - p, 0, False)
                transpose1(n, 1, lead)
                prob_values1(n, p, 0, lead)
                if not is_last:
                    score1(n + 1, 1 - p, 1, False)
                transpose1(n, 2, lead)
                prob_values1(n, p, 1, lead)
                if not is_first:
                    turn_back(n - 1, False)
                if not is_last:
                    score1(n + 1, 1 - p, 2, False)
                transpose1(n, 3, lead)
                prob_values1(n, p, 2, lead, END_O[1] if is_last else END_O[0])
                if is_last:
                    turn_back_half(n, a, 0)
                    prob_values1(n, p, 3, lead, END_O[1])
                    attention_T(n, a, 0)
                    seed("b_proj" if a == 0 else "b_out", 0)
                    seed("b_proj" if a == 0 else "b_out", 1)
                    turn_back_half(n, a, 1)
                    project_out1(a, 0)
                    attention_T(n, a, 1)
                    keep_warm(4, 2)
                    project_out1(a, 1)
                    keep_warm(8, 2)

            def turn_back_half(n, a, half):
                if half == 0:
                    pe.wait_ge(end_ev, a + 1)
                    pe.wait_ge(a_norm, n)
                else:
                    pe.wait_ge(a_ev, n + 1)
                nc.tensor.transpose(bank[END_BACK[half]][:, bcols(half)], oS[:, bcols(half)], ident).then_inc(
                    a_back if half else end_back, 1)

            def attention_T(n, a, half):
                pe.wait_ge(*((a_norm, n + 1) if half else (end_norm, a + 1)))
                pe.wait_ge(a_Tc[half], (n + 1) * 2)
                for u in range(HALF):
                    last = nc.tensor.transpose(bank[4 + half][:, bcols(u)], oN[:, HALF * half + u, :], ident)
                last.then_inc(post_T, 1)

            def project_out1(a, half):
                w = wsq[:, SQ["proj" if a == 0 else "out"] * P:][:, 0:P]
                pe.wait_ge(post_oT, 2 * a + half + 1)
                for u in range(HALF):
                    last = mm(bank[6 + half][:, bcols(u)], oT[:, bcols(HALF * half + u)], w, False, False)
                last.then_inc(acc_done, 1)

            def mlp(k, name):
                base = 0 if k == 2 else 2 * FF
                off = 0 if k == 2 else 2 * FF * P

                def up(half, c):
                    j = FF * half + c
                    if c == 0:
                        wait_hT(k, half)
                    if j >= 4:
                        pe.wait_ge(ffn_g, base + j - 3)
                    mm(bank[MLP_BANKS[j % 4]][:, :], wff[:, off + c * P:off + (c + 1) * P],
                       hT[:, half * BANK:(half + 1) * BANK], True, True).then_inc(ffn_h, 1)

                def down(half):
                    pe.wait_ge(x_sum, 2 * k - 1 + half)
                    seed(name, half)
                    for c in range(FF):
                        pe.wait_ge(ffn_g, base + FF * half + c + 1)
                        for u in range(HALF):
                            last = mm(bank[6 + half][:, bcols(u)], gT[:, c, bcols(HALF * half + u)],
                                      wff[:, off + (FF + c) * P:off + (FF + c + 1) * P], False, False)
                    last.then_inc(acc_done, 1)

                transpose_norm(k, 0)
                keep_warm(3, 0)
                for c in range(FF - 1):
                    up(0, c)
                transpose_norm(k, 1)
                up(0, FF - 1)
                up(1, 0)
                down(0)
                for c in range(1, FF):
                    up(1, c)
                down(1)

            def modulation(stage):
                j0, j1 = MOD_STAGES[stage]
                for j in range(j0, j1):
                    last = mm(bank[MOD_BANKS[stage]][:, (j - j0) * B:(j - j0 + 1) * B], wmod[:, bcols(j)],
                              condT if j < 4 else silu[:, 3, :], True, True)
                last.then_inc(mod_ps, 1)

            pe.wait_ge(presets, 2)
            keep_warm(14, 7)
            pe.wait_ge(ld_small, 16)
            pe.wait_ge(ld_mod, 16)
            pe.wait_ge(silu_done, 1)
            modulation(0)
            keep_warm(6, 7)
            for a in range(2):
                transpose_norm(a, 0)
                keep_warm(3, 0)
                for f in (range(6) if a == 0 else (0, 2)):
                    if f == 2:
                        if a:
                            keep_warm(4, 0)
                        transpose_norm(a, 1)
                        keep_warm(4, 7)
                    fill(STEPS * a, f, 0, a, k=a, ps=FIRST_BANKS[f])
                if a == 0:
                    modulation(1)
                head_pairs(pe, STEPS * a, partial(l0_step, a=a))
            pe.wait_ge(ld_ff, 16)
            mlp(2, "ff_b2")
            for a in range(2):
                transpose_norm(3 + a, 0)
                keep_warm(3, 0)
                for j in range(NPRE[a], NPRE[a + 1]):
                    if PRE[j][1] and not PRE[j - 1][1]:
                        transpose_norm(3 + a, 1)
                        keep_warm(4, 7)
                    pre_fill(j)
                head_pairs(pe, STEPS * a, partial(l1_step, a=a))
            mlp(5, "b_fc2")


def _packed(i):
    def pad(w):
        return np.concatenate([w, np.zeros((P - w.shape[0], *w.shape[1:]), w.dtype)], axis=0)

    wqkv = []
    for wq, wkv in (("sa_wq", "sa_wkv"), ("ca_wq", "ca_wkv")):
        q, kv = i["L0_xcond_" + wq], pad(i["L0_xcond_" + wkv])
        for s in range(STEPS):
            c = slice(P * s, P * (s + 1))
            wqkv.append(np.concatenate([q[:, c], kv[:, c], kv[:, H * DH0:][:, c]], axis=1))
    wqkv.append(np.zeros_like(wqkv[0]))
    wo = np.concatenate([i["L0_xcond_sa_wo"].reshape(STEPS, P, P), i["L0_xcond_ca_wo"].reshape(STEPS, P, P)], axis=0)
    ada = [i["L1_xcond_W_ada"][:, P * j:P * (j + 1)] for j in (1, 0, 3, 2, 5, 4)]
    wmod = np.concatenate([i["L0_xcond_g1_w"], i["L0_xcond_b1_w"], i["L0_xcond_g2_w"], i["L0_xcond_b2_w"], *ada], axis=1)
    wsq = np.concatenate([i["L1_xcond_W_qkv"], i["L1_xcond_W_proj"], i["L1_xcond_W_q"], i["L1_xcond_W_k"],
                          i["L1_xcond_W_v"], i["L1_xcond_W_out"], pad(i["L1_xcond_W_ctx"])], axis=1)

    def down(w):
        return w.reshape(FF, P, P).transpose(1, 0, 2).reshape(P, FF * P)

    wff = np.concatenate([i["L0_xcond_ff_w1"], down(i["L0_xcond_ff_w2"]), i["L1_xcond_W_fc1"], down(i["L1_xcond_W_fc2"])],
                         axis=1)
    bqkv = i["L1_xcond_b_qkv"].reshape(3, P)
    b_ada = i["L1_xcond_b_ada"].reshape(6, P)
    vecs = [i["L0_xcond_" + n] for n in ("g1_b", "b1_b", "g2_b", "b2_b")] + [b_ada[j] for j in (1, 0, 3, 2, 5, 4)]
    vecs += [i["L0_xcond_" + n] for n in ("ln1_w", "ln1_b", "ln2_w", "ln2_b")]
    vecs += [pad(i["L0_xcond_ca_lnc_w"]), pad(i["L0_xcond_ca_lnc_b"]), bqkv[0], bqkv[1], bqkv[2], i["L1_xcond_b_ctx"]]
    vecs += list(i["L0_xcond_ff_b1"].reshape(FF, P)) + list(i["L1_xcond_b_fc1"].reshape(FF, P))
    rows = np.concatenate([i["L0_xcond_sa_bo"], i["L0_xcond_ca_bo"], i["L0_xcond_ff_b2"], i["L1_xcond_b_proj"],
                           i["L1_xcond_b_out"], i["L1_xcond_b_fc2"]]).reshape(-1, P)
    chan = np.arange(P) % DH0
    inv = (np.float32(1.0) / np.float32(10000.0) ** (np.arange(0, DH0, 2, dtype=np.float32) / np.float32(DH0)))
    ang = (np.arange(P, dtype=np.float32)[:, None] * inv.astype(np.float32)[None, :]).astype(np.float32)
    cos, sin = np.cos(ang).T[chan // 2], np.sin(ang).T[chan // 2]
    sin = np.where(chan[:, None] % 2 == 0, -sin, sin)
    mask = (np.arange(P)[:, None] // DH1 == np.arange(H)[None, :])
    const = np.concatenate([np.eye(P), cos, sin, mask], axis=1).astype(np.float32)
    small = np.concatenate([const, i["cond_1024"].T, np.stack(vecs, axis=1)], axis=1)
    return {
        "small": small, "x": i["x"], "ctx": i["ctx_768"], "ctxT": i["ctx_768"].reshape(B * P, DC).T,
        "wqkv": np.stack(wqkv), "wo": wo, "wmod": wmod, "wsq": wsq, "wff": wff, "row": rows,
    }


def kernel(**inputs):
    import concourse.bacc as bacc
    from concourse.bass_utils import run_bass_kernel_spmd

    nc = bacc.Bacc("TRN2", target_bir_lowering=False, num_devices=1)
    arrays, args = {}, []
    for name, a in _packed({k: np.asarray(v) for k, v in inputs.items()}).items():
        arrays[f"in_{name}"] = np.ascontiguousarray(a)
        args.append(nc.dram_tensor(f"in_{name}", a.shape, F32, kind="ExternalInput").ap())
    args.append(nc.dram_tensor("out_x", (B, P, P), F32, kind="ExternalOutput").ap())
    build(nc, *args)
    return run_bass_kernel_spmd(nc, [arrays], core_ids=[0]).results[0]["out_x"]
```
